# Optimizing a Trainium2 kernel written in Bass

```python
import numpy as np
import jax
import jax.numpy as jnp

def _softmax(x, axis=-1):
    return jax.nn.softmax(x, axis=axis)

def _gelu(x):
    return jax.nn.gelu(x, approximate=True)

def _silu(x):
    return jax.nn.silu(x)

def _sigmoid(x):
    return jax.nn.sigmoid(x)

def _layernorm(x, axis=-1, eps=1e-05):
    m = jnp.mean(x, axis=axis, keepdims=True)
    v = jnp.var(x, axis=axis, keepdims=True)
    return (x - m) / jnp.sqrt(v + eps)

def _scatter_add(tgt, idx, src, axis=0):
    return tgt.at[idx].add(src)

def _segment_sum(src, seg, n):
    return jax.ops.segment_sum(src, seg, n)
kernel_name = 'mk_gnn_resnorm_d4_gnn_r8_cf7510'

def setup_inputs(seed: int=0):
    np.random.seed(seed)
    _w = jnp.asarray

    def _rec_inputs():
        import jax
        import jax.numpy as jnp
        _gk = jax.random.key(seed)
        x = -0.0005121 + 1.001 * jax.random.normal(jax.random.fold_in(_gk, 1), (6250, 64), jnp.float32)
        _s = jax.random.randint(jax.random.fold_in(_gk, 2), (100000,), 0, 6250, jnp.int32)
        _d = jax.random.randint(jax.random.fold_in(_gk, 3), (100000,), 0, 6250, jnp.int32)
        _loop = jnp.arange(6250, dtype=jnp.int32)
        src = jnp.concatenate([_s, _d, _loop])
        dst = jnp.concatenate([_d, _s, _loop])
        _o = jnp.argsort(dst, stable=True)
        src = src[_o]
        dst = dst[_o]
        edge_attr_16 = 0.000216709 + 1.00012 * jax.random.normal(jax.random.fold_in(_gk, 11), (206250, 16), jnp.float32)
        edge_attr_64 = -6.74381e-05 + 0.999835 * jax.random.normal(jax.random.fold_in(_gk, 12), (206250, 64), jnp.float32)
        edge_weight = jax.random.uniform(jax.random.fold_in(_gk, 14), (206250,), jnp.float32, 0.0, 0.999999)
        return (x, src, dst, edge_attr_16, edge_attr_64, edge_weight)
    x, src, dst, edge_attr_16, edge_attr_64, edge_weight = _rec_inputs()

    def _L0_gnn_setup():
        import jax, jax.numpy as jnp
        import numpy as np
        N = 6250
        E = 100000
        D_IN = 64
        D_HID = 128
        D_OUT = 64

        def gin_conv(x, W, b, src, dst):
            agg = jax.ops.segment_sum(x[src], dst, num_segments=N)
            return (x + agg) @ W + b
        key = jax.random.key(seed)
        k1, k2, k3, k4, k5, k6, k7 = jax.random.split(key, 7)
        x = jax.random.normal(k1, (N, D_IN), dtype=jnp.float32)
        edge_index = jax.random.randint(k2, (2, E), 0, N, dtype=jnp.int64 if jax.config.jax_enable_x64 else jnp.int32)
        W1 = jax.random.normal(k3, (D_IN, D_HID), dtype=jnp.float32) * (1.0 / np.sqrt(D_IN))
        b1 = jax.random.normal(k4, (D_HID,), dtype=jnp.float32) * 0.01
        W2 = jax.random.normal(k5, (D_HID, D_OUT), dtype=jnp.float32) * (1.0 / np.sqrt(D_HID))
        b2 = jax.random.normal(k6, (D_OUT,), dtype=jnp.float32) * 0.01
        return {'x': x, 'W1': W1, 'b1': b1, 'W2': W2, 'b2': b2, 'edge_index': edge_index}
    _L0_gnn_all = _L0_gnn_setup()
    _L0_gnn_in = {k: v for k, v in _L0_gnn_all.items() if k in ('W1', 'b1', 'W2', 'b2')}
    del _L0_gnn_all

    def _L1_gnn_setup():
        import jax, jax.numpy as jnp
        import numpy as np
        N_NODES = 6250
        N_EDGES = 156250
        D_FEAT = 64
        key = jax.random.key(seed)
        k1, k2, k3 = jax.random.split(key, 3)
        x = jax.random.normal(k1, (N_NODES, D_FEAT), dtype=jnp.float32)
        edge_attr = jax.random.normal(k2, (N_EDGES, D_FEAT), dtype=jnp.float32)
        edge_index = jax.random.randint(k3, (2, N_EDGES), 0, N_NODES, dtype=jnp.int64)
        return {'x': x, 'edge_attr': edge_attr, 'edge_index': edge_index}
    _L1_gnn_all = _L1_gnn_setup()
    _L1_gnn_in = {k: v for k, v in _L1_gnn_all.items() if k in ()}
    del _L1_gnn_all

    def _L2_gnn_setup():
        import jax, jax.numpy as jnp
        import numpy as np
        N = 12500
        E = 200000
        F_IN = 64
        F_HID = 128
        F_EDGE = 16
        CUTOFF = 5.0
        IN_DIM = 2 * F_IN + F_EDGE + 1
        key = jax.random.key(seed)
        ks = jax.random.split(key, 12)

        def lin(k, fan_in, fan_out):
            bound = 1.0 / np.sqrt(fan_in)
            kw, kb = jax.random.split(k)
            W = jax.random.uniform(kw, (fan_in, fan_out), jnp.float32, -bound, bound)
            b = jax.random.uniform(kb, (fan_out,), jnp.float32, -bound, bound)
            return (W, b)
        x = jax.random.normal(ks[0], (N, F_IN), jnp.float32)
        edge_index = jax.random.randint(ks[1], (2, E), 0, N, jnp.int32)
        edge_weight = jax.random.uniform(ks[2], (E,), jnp.float32)
        edge_attr = jax.random.normal(ks[3], (E, F_EDGE), jnp.float32)
        ew1, eb1 = lin(ks[4], IN_DIM, F_HID)
        ew2, eb2 = lin(ks[5], F_HID, F_HID)
        nw1, nb1 = lin(ks[6], F_IN + F_HID, F_HID)
        nw2, nb2 = lin(ks[7], F_HID, F_IN)
        return {'x': x, 'edge_index': edge_index, 'edge_weight': edge_weight, 'edge_attr': edge_attr, 'ew1': ew1, 'eb1': eb1, 'ew2': ew2, 'eb2': eb2, 'nw1': nw1, 'nb1': nb1, 'nw2': nw2, 'nb2': nb2}
    _L2_gnn_all = _L2_gnn_setup()
    _L2_gnn_in = {k: v for k, v in _L2_gnn_all.items() if k in ('ew1', 'eb1', 'ew2', 'eb2', 'nw1', 'nb1', 'nw2', 'nb2')}
    del _L2_gnn_all

    def _L3_gnn_setup():
        import jax, jax.numpy as jnp
        import numpy as np
        N_NODES = 12500
        N_EDGES = 200000
        EMB_DIM = 64
        key = jax.random.key(seed)
        k1, k2, k3, k4, k5, k6 = jax.random.split(key, 6)
        x = jax.random.normal(k1, (N_NODES, EMB_DIM), dtype=jnp.float32)
        edge_index = jax.random.randint(k2, (2, N_EDGES), 0, N_NODES, dtype=jnp.int64)
        scale = 1.0 / np.sqrt(EMB_DIM)
        W1 = jax.random.normal(k3, (EMB_DIM, EMB_DIM), dtype=jnp.float32) * scale
        b1 = jax.random.normal(k4, (EMB_DIM,), dtype=jnp.float32) * scale
        W2 = jax.random.normal(k5, (EMB_DIM, EMB_DIM), dtype=jnp.float32) * scale
        b2 = jax.random.normal(k6, (EMB_DIM,), dtype=jnp.float32) * scale
        return {'x': x, 'edge_index': edge_index, 'W1': W1, 'b1': b1, 'W2': W2, 'b2': b2}
    _L3_gnn_all = _L3_gnn_setup()
    _L3_gnn_in = {k: v for k, v in _L3_gnn_all.items() if k in ('W1', 'b1', 'W2', 'b2')}
    del _L3_gnn_all
    return {'x': x, 'src': src, 'dst': dst, 'edge_attr_16': edge_attr_16, 'edge_attr_64': edge_attr_64, 'edge_weight': edge_weight, 'L0_gnn_W1': _L0_gnn_in['W1'], 'L0_gnn_b1': _L0_gnn_in['b1'], 'L0_gnn_W2': _L0_gnn_in['W2'], 'L0_gnn_b2': _L0_gnn_in['b2'], 'L2_gnn_ew1': _L2_gnn_in['ew1'], 'L2_gnn_eb1': _L2_gnn_in['eb1'], 'L2_gnn_ew2': _L2_gnn_in['ew2'], 'L2_gnn_eb2': _L2_gnn_in['eb2'], 'L2_gnn_nw1': _L2_gnn_in['nw1'], 'L2_gnn_nb1': _L2_gnn_in['nb1'], 'L2_gnn_nw2': _L2_gnn_in['nw2'], 'L2_gnn_nb2': _L2_gnn_in['nb2'], 'L3_gnn_W1': _L3_gnn_in['W1'], 'L3_gnn_b1': _L3_gnn_in['b1'], 'L3_gnn_W2': _L3_gnn_in['W2'], 'L3_gnn_b2': _L3_gnn_in['b2']}

def reference(x, src, dst, edge_attr_16, edge_attr_64, edge_weight, L0_gnn_W1, L0_gnn_b1, L0_gnn_W2, L0_gnn_b2, L2_gnn_ew1, L2_gnn_eb1, L2_gnn_ew2, L2_gnn_eb2, L2_gnn_nw1, L2_gnn_nb1, L2_gnn_nw2, L2_gnn_nb2, L3_gnn_W1, L3_gnn_b1, L3_gnn_W2, L3_gnn_b2):
    import jax
    import jax.numpy as jnp

    def _L0_gnn_ref(x, W1, b1, W2, b2, edge_index):
        import jax, jax.numpy as jnp
        import numpy as np
        N = 6250
        E = 100000
        D_IN = 64
        D_HID = 128
        D_OUT = 64

        def gin_conv(x, W, b, src, dst):
            agg = jax.ops.segment_sum(x[src], dst, num_segments=N)
            return (x + agg) @ W + b
        src, dst = (edge_index[0], edge_index[1])
        h = gin_conv(x, W1, b1, src, dst)
        h = jax.nn.relu(h)
        out = gin_conv(h, W2, b2, src, dst)
        return out

    def _L1_gnn_ref(x, edge_attr, edge_index):
        import jax, jax.numpy as jnp
        import numpy as np
        N_NODES = 6250
        N_EDGES = 156250
        D_FEAT = 64
        src = edge_index[0]
        dst = edge_index[1]
        messages = x[src] + x[dst] + edge_attr
        out = jax.ops.segment_sum(messages, dst, num_segments=x.shape[0])
        return out

    def _L2_gnn_ref(x, edge_index, edge_weight, edge_attr, ew1, eb1, ew2, eb2, nw1, nb1, nw2, nb2):
        import jax, jax.numpy as jnp
        import numpy as np
        N = 12500
        E = 200000
        F_IN = 64
        F_HID = 128
        F_EDGE = 16
        CUTOFF = 5.0
        IN_DIM = 2 * F_IN + F_EDGE + 1
        row, col = (edge_index[0], edge_index[1])
        d_raw = (edge_weight / CUTOFF)[:, None]
        edge_input = jnp.concatenate([x[row], x[col], edge_attr, d_raw], axis=-1)
        h = jax.nn.silu(edge_input @ ew1 + eb1)
        m_ij = jax.nn.silu(h @ ew2 + eb2)
        agg = jax.ops.segment_sum(m_ij, row, num_segments=x.shape[0])
        node_in = jnp.concatenate([x, agg], axis=-1)
        upd = jax.nn.silu(node_in @ nw1 + nb1) @ nw2 + nb2
        return x + upd

    def _L3_gnn_ref(x, edge_index, W1, b1, W2, b2):
        import jax, jax.numpy as jnp
        import numpy as np
        N_NODES = 12500
        N_EDGES = 200000
        EMB_DIM = 64
        row, col = (edge_index[0], edge_index[1])
        n = x.shape[0]
        deg = jax.ops.segment_sum(jnp.ones_like(col, dtype=x.dtype), col, num_segments=n)
        deg_inv_sqrt = jnp.where(deg > 0, jax.lax.rsqrt(jnp.maximum(deg, 1.0)), 0.0)
        norm = deg_inv_sqrt[row] * deg_inv_sqrt[col]
        xr = x[row]
        xc = x[col]
        msg = norm[:, None] * (xc @ W1.T + b1 + xr * xc @ W2.T + b2)
        agg = jax.ops.segment_sum(msg, row, num_segments=n)
        return jax.nn.leaky_relu(agg, negative_slope=0.2)
    edge_index = jnp.stack([src, dst])
    x = _layernorm(x + _L0_gnn_ref(x, L0_gnn_W1, L0_gnn_b1, L0_gnn_W2, L0_gnn_b2, edge_index), axis=-1)
    x = _layernorm(x + _L1_gnn_ref(x, edge_attr_64, edge_index), axis=-1)
    x = _layernorm(x + _L2_gnn_ref(x, edge_index, edge_weight, edge_attr_16, L2_gnn_ew1, L2_gnn_eb1, L2_gnn_ew2, L2_gnn_eb2, L2_gnn_nw1, L2_gnn_nb1, L2_gnn_nw2, L2_gnn_nb2), axis=-1)
    x = _layernorm(x + _L3_gnn_ref(x, edge_index, L3_gnn_W1, L3_gnn_b1, L3_gnn_W2, L3_gnn_b2), axis=-1)
    return x

_drawn_inputs = setup_inputs


def setup_inputs(seed=0):
    import zlib

    import numpy as np

    out = dict(_drawn_inputs(seed))
    spreads = {}
    factors = {'edge_attr_16': 5.652,
     'edge_weight': 200.0,
     'L0_gnn_b1': 27.498,
     'L0_gnn_b2': 200.0,
     'L2_gnn_nb1': 6.245,
     'L2_gnn_nb2': 2.754}
    for name, (base, spread) in spreads.items():
        noise = np.random.default_rng([zlib.crc32(name.encode()), seed]).standard_normal(out[name].shape)
        drawn = base * np.exp(spread * noise) if base else spread * noise
        out[name] = jnp.asarray(drawn.astype(out[name].dtype))
    for name, factor in factors.items():
        out[name] = (out[name] * factor).astype(out[name].dtype)
    return out
```

```python
from contextlib import ExitStack

import concourse.bass as bass
from concourse import mybir

P = 128
N = 6250
E = 206250
F = 64
H = 128
FE = 16
NB = -(-N // P)
TAIL = N - (NB - 1) * P
EP = 125
EC = E // EP
G = 4
SLOTS = 4
STEP = G * SLOTS
CHUNKS = -(-((E + NB * (P - 1)) // P) // STEP) * STEP
ITERS = CHUNKS // STEP
SC = 15
SITERS = EC // (2 * SC)
IN_REC = 68
OUT_REC = 32
XW = F + IN_REC
EPS = 1e-5
CUTOFF = 5.0
NODE_B = 7
NODE_STEPS = NB // NODE_B
PRE = 16

assert EP * EC == E and EC % (2 * SC) == 0 and NB == NODE_B * NODE_STEPS and CHUNKS % PRE == 0

ALU = mybir.AluOpType
ACT = mybir.ActivationFunctionType
AX_X = mybir.AxisListType.X
F32 = mybir.dt.float32
BF16 = mybir.dt.bfloat16
I32 = mybir.dt.int32
DVE = mybir.EngineType.DVE
SP = mybir.EngineType.SP
ds = bass.ds


class Chain:

    def __init__(self, eng, sem):
        self.eng, self.sem, self.n = eng, sem, 0

    def __call__(self, ins):
        ins.then_inc(self.sem, 1)
        self.n += 1
        self.eng.wait_ge(self.sem, self.n)


class Stage:

    def __init__(self, nc, ctx, name):
        self.nc, self.ctx, self.name, self.signals = nc, ctx, name, []

    def sb(self, name, shape, dt=F32):
        return self.ctx.enter_context(self.nc.sbuf_tensor(f"{self.name}_{name}", shape, dt))

    def ps(self, name, shape):
        return self.ctx.enter_context(self.nc.psum_tensor(f"{self.name}_{name}", shape, F32))

    def sem(self, name):
        self.signals.append(self.ctx.enter_context(self.nc.semaphore(f"{self.name}_{name}")))
        return self.signals[-1]

    def sems(self, name):
        return [self.sem(f"{name}{s}") for s in range(SLOTS)]

    def block(self):
        self.ctx.callback(self.clear)
        return self.ctx.enter_context(self.nc.Block())

    def clear(self):
        with self.nc.Block() as block:
            @block.gpsimd
            def _(pool):
                for signal in self.signals:
                    pool.sem_clear(signal)


def steps(eng, n):
    yield 0
    with eng.Fori(1, n) as i:
        yield i


def wait_count(eng, sem, count):
    if not isinstance(count, int) or count > 0:
        eng.wait_ge(sem, count)


def turnstile(pool, gate, slot, passed):
    pool.tensor_tensor(gate[0:1, slot + 1:slot + 2], gate[0:1, 0:1], gate[0:1, 0:1], ALU.mult).then_inc(passed, 1)


def bc(ap, dim, n):
    return ap.unsqueeze(dim).to_broadcast([*ap.shape[:dim], n, *ap.shape[dim:]])


def constants(nc, k):
    with ExitStack() as ctx:
        st = Stage(nc, ctx, "constants")
        sb, ps, sem, sems = st.sb, st.ps, st.sem, st.sems
        s_ones = sem("ones_set")
        s_sel = sem("masks_set")
        block = st.block()

        @block.gpsimd
        def _(pool):
            nc.gpsimd.memset(k["ones"][:], 1.0).then_inc(s_ones, 1)
            nc.gpsimd.memset(k["gate"][:], 0.0)
            nc.gpsimd.iota(k["iota"][:], [[1, P]], base=0, channel_multiplier=0,
                           allow_small_or_imprecise_dtypes=True)
            nc.gpsimd.iota(k["chunk_start"][:], [[P, CHUNKS]], base=0, channel_multiplier=0)
            pool.wait_ge(s_ones, 1)
            nc.gpsimd.affine_select(out=k["ident"][:], in_=k["ones"][:], compare_op=ALU.is_equal, fill=0.0,
                                    base=0, pattern=[[-1, P]], channel_multiplier=1).then_inc(s_sel, 1)
            nc.gpsimd.affine_select(out=k["before"][:], in_=k["ones"][:], compare_op=ALU.is_gt, fill=0.0,
                                    base=0, pattern=[[1, P]], channel_multiplier=-1).then_inc(s_sel, 1)
            nc.gpsimd.memset(k["zeros"][:], 0.0).then_inc(s_sel, 1)
            pool.wait_ge(s_sel, 3)


def sort_edges(nc, k, src, dst, ea16, ea64, weight, in_rec, out_rec):
    with ExitStack() as ctx:
        st = Stage(nc, ctx, "sort")
        sb, ps, sem, sems = st.sb, st.ps, st.sem, st.sems
        ends = {"in": sb("dst_all", [EP, EC], I32), "out": sb("src_all", [EP, EC], I32)}
        wts = sb("weight_all", [EP, EC])
        low = {o: sb(f"low_{o}", [EP, EC]) for o in ends}
        row = {o: sb(f"row_{o}", [EP, EC], I32) for o in ends}
        ints = sb("ints", [EP, EC], I32)
        blk = sb("blk", [EP, EC])
        eq = sb("eq", [EP, EC])
        run = sb("run", [EP, EC])
        zeros = sb("zeros", [EP, EC])
        pos = sb("pos", [EP, EC])
        count = sb("count", [EP, NB])
        total = sb("total", [P, NB])
        padded = sb("padded", [P, NB])
        padded_i = sb("padded_i", [P, NB], I32)
        upto = sb("upto", [P, NB])
        first = sb("first", [P, NB])
        offset = sb("offset", [EP, NB])
        first_col = sb("first_col", [NB, 1])
        after = sb("after", [NB, CHUNKS])
        in_default = sb("in_default", [P, PRE, IN_REC])
        out_default = sb("out_default", [P, PRE, OUT_REC])
        recs = {"in": [sb(f"in_recs{s}", [EP, SC, IN_REC]) for s in range(2)],
                "out": [sb(f"out_recs{s}", [EP, SC, OUT_REC]) for s in range(2)]}
        rows = {o: [sb(f"rows_{o}{s}", [EP, SC], I32) for s in range(2)] for o in ends}
        p_off = ps("p_off", [P, 512])
        p_tot = ps("p_tot", [P, 512])
        p_col = ps("p_col", [P, 512])
        p_blk = ps("p_blk", [1, 4, 512])

        loaded = sem("edges_loaded")
        defaults_set = sem("defaults_set")
        prefilled = sem("scratch_prefilled")
        chain = sem("sort_chain")
        counted = sem("counted")
        scaled = sem("weights_scaled")
        offsets_made = sem("offsets_made")
        first_made = sem("first_made")
        col_made = sem("col_made")
        after_made = sem("after_made")
        blk_summed = sem("blk_summed")
        rows_made = sem("rows_made")
        rec_zero = sem("rec_buffers_set")
        attr_in = {o: [sem(f"attr_{o}{s}") for s in range(2)] for o in ends}
        staged = {o: [sem(f"staged_{o}{s}") for s in range(2)] for o in ends}
        scattered = {"in": k["dma_scatter"][0:2], "out": k["dma_scatter"][2:4]}
        passed = {o: [sem(f"passed_{o}{s}") for s in range(2)] for o in ends}
        order = ("in", "out")
        other = {"in": "out", "out": "in"}
        attrs = {"in": ea64.rearrange("(p c) w -> p c w", p=EP), "out": ea16.rearrange("(p c) w -> p c w", p=EP)}
        width = {"in": F, "out": FE}
        in_rows = in_rec.rearrange("(p c) w -> p c w", p=P)
        out_rows = out_rec.rearrange("(p c) w -> p c w", p=P)
        block = st.block()

        @block.sync
        def _(sp):
            sp.dma_start(ends["in"][:], dst.rearrange("(p c) -> p c", p=EP)).then_inc(loaded, 16)
            sp.dma_start(ends["out"][:], src.rearrange("(p c) -> p c", p=EP)).then_inc(loaded, 16)
            sp.dma_start(wts[:], weight.rearrange("(p c) -> p c", p=EP)).then_inc(loaded, 16)
            sp.wait_ge(defaults_set, 4)
            for i in steps(sp, CHUNKS // PRE):
                sp.dma_start(in_rows[:, ds(i * PRE, PRE)], in_default[:]).then_inc(prefilled, 16)
                sp.dma_start(out_rows[:, ds(i * PRE, PRE)], out_default[:]).then_inc(prefilled, 16)
            for o in order:
                sp.wait_ge(rec_zero, 6)
                for i in steps(sp, SITERS):
                    for s in range(2):
                        wait_count(sp, scattered[o][s], i * (16 * SC))
                        sp.dma_start(recs[o][s][:, :, 0:width[o]],
                                     attrs[o][:, ds(i * (2 * SC) + s * SC, SC)]).then_inc(attr_in[o][s], 16)

        @block.gpsimd
        def _(pool):
            nc.gpsimd.memset(in_default[:], 0.0).then_inc(defaults_set, 1)
            nc.gpsimd.memset(out_default[:], 0.0).then_inc(defaults_set, 1)
            pool.wait_ge(defaults_set, 2)
            nc.gpsimd.memset(in_default[:, :, F + 2:F + 3], -1.0).then_inc(defaults_set, 1)
            nc.gpsimd.memset(out_default[:, :, FE + 2:FE + 3], -1.0).then_inc(defaults_set, 1)
            for s in range(2):
                nc.gpsimd.memset(recs["in"][s][:], 1.0).then_inc(rec_zero, 1)
                nc.gpsimd.memset(recs["out"][s][:], 0.0).then_inc(rec_zero, 1)
            nc.gpsimd.memset(zeros[:], 0.0).then_inc(rec_zero, 1)
            nc.gpsimd.memset(pos[:], 0.0).then_inc(rec_zero, 1)
            dest = {"in": in_rec, "out": out_rec}
            for n, o in enumerate(order):
                for i in steps(pool, SITERS):
                    for s in range(2):
                        pool.wait_ge(attr_in[o][s], i * 16 + 16)
                        pool.wait_ge(staged[o][s], i * 3 + 3)
                        pool.wait_ge(prefilled, 32 * (CHUNKS // PRE))
                        turnstile(pool, k["gate"], 2 * n + s, passed[o][s])
                        for c in range(SC):
                            pool.indirect_dma_start(
                                out=dest[o], out_offset=bass.IndirectOffsetOnAxis(ap=rows[o][s][:, c:c + 1], axis=0),
                                in_=recs[o][s][:, c], in_offset=None).then_inc(scattered[o][s], 16)
            for o in order:
                for s in range(2):
                    pool.wait_ge(scattered[o][s], SITERS * 16 * SC)

        @block.scalar
        def _(act):
            act.wait_ge(loaded, 48)
            act.wait_ge(rec_zero, 6)
            act.wait_ge(scaled, 1)
            for n, o in enumerate(order):
                act.wait_ge(rows_made, n + 1)
                for i in steps(act, SITERS):
                    for s in range(2):
                        wait_count(act, scattered[o][s], i * (16 * SC))
                        wait_count(act, passed[o][s], i)
                        at = ds(i * (2 * SC) + s * SC, SC)
                        far = recs[o][s][:, :, width[o] + 1].bitcast(I32)
                        act.copy(far, ends[other[o]][:, at]).then_inc(staged[o][s], 1)
                        act.copy(recs[o][s][:, :, width[o] + 2], low[o][:, at]).then_inc(staged[o][s], 1)
                        if o == "out":
                            act.copy(recs[o][s][:, :, FE], wts[:, at])
                        act.copy(rows[o][s][:], row[o][:, at]).then_inc(staged[o][s], 1)

        @block.tensor
        def _(pe):
            for n, o in enumerate(order):
                pe.wait_ge(counted, n + 1)
                pe.matmul(p_off[0:EP, 0:NB], k["before"][0:EP, 0:EP], count[:], start=True, stop=True)
                pe.matmul(p_tot[:, 0:NB], k["ones"][0:EP, :], count[:], start=True, stop=True).then_inc(offsets_made, 1)
                pe.wait_ge(first_made, n + 1)
                pe.transpose(p_col[0:NB, 0:1], first[0:1, :], k["ident"][0:1, 0:1]).then_inc(col_made, 1)
                pe.wait_ge(after_made, n + 1)
                for q in range(4):
                    w = CHUNKS // 4
                    mm = pe.matmul(p_blk[:, q, 0:w], k["ones"][0:NB, 0:1], after[:, q * w:(q + 1) * w],
                                   start=True, stop=True)
                mm.then_inc(blk_summed, 1)

        @block.vector
        def _(dve):
            step = Chain(dve, chain)
            dve.wait_ge(loaded, 48)
            dve.wait_ge(rec_zero, 6)
            dve.tensor_scalar(wts[:], wts[:], 1.0 / CUTOFF, None, ALU.mult).then_inc(scaled, 1)
            for n, o in enumerate(order):
                step(dve.tensor_scalar(ints[:], ends[o][:], P - 1, None, ALU.bitwise_and))
                step(dve.tensor_copy(low[o][:], ints[:]))
                step(dve.tensor_scalar(ints[:], ends[o][:], 7, None, ALU.logical_shift_right))
                step(dve.tensor_copy(blk[:], ints[:]))
                for b in steps(dve, NB):
                    dve.tensor_scalar(eq[:], blk[:], k["iota"][0:EP, ds(b, 1)], 0.0, ALU.is_equal, ALU.add,
                                      accum_out=count[:, ds(b, 1)]).then_inc(chain, 1)
                    dve.wait_ge(chain, b + (step.n + 1))
                step.n += NB
                dve.tensor_copy(pos[:], zeros[:]).then_inc(counted, 1)
                dve.wait_ge(counted, n + 1)
                dve.wait_ge(offsets_made, n + 1)
                step(dve.tensor_scalar(padded_i[:], p_tot[:, 0:NB], float(P - 1), None, ALU.add))
                step(dve.tensor_scalar(padded_i[:], padded_i[:], 7, 7, ALU.logical_shift_right,
                                       ALU.arith_shift_left))
                step(dve.tensor_copy(padded[:], padded_i[:]))
                step(dve.tensor_tensor_scan(upto[:], padded[:], k["zeros"][:, 0:NB], 0.0, ALU.add, ALU.add))
                step(dve.tensor_tensor(first[:], upto[:], padded[:], ALU.subtract))
                dve.scalar_tensor_tensor(out=offset[:], in0=p_off[0:EP, 0:NB], scalar=-1.0, in1=first[0:EP, :],
                                         op0=ALU.add, op1=ALU.add).then_inc(first_made, 1)
                dve.wait_ge(first_made, n + 1)
                dve.wait_ge(col_made, n + 1)
                step(dve.tensor_copy(first_col[:], p_col[0:NB, 0:1]))
                dve.tensor_scalar(after[:], k["chunk_start"][0:NB, :], first_col[:, 0:1], None,
                                  ALU.is_ge).then_inc(after_made, 1)
                dve.wait_ge(blk_summed, n + 1)
                step(dve.tensor_scalar(k["blk_" + o][:].rearrange("p (q w) -> p q w", q=4),
                                       p_blk[:, :, 0:CHUNKS // 4], -1.0, None, ALU.add))
                for b in steps(dve, NB):
                    dve.tensor_scalar(eq[:], blk[:], k["iota"][0:EP, ds(b, 1)], None, ALU.is_equal).then_inc(chain, 1)
                    dve.wait_ge(chain, b * 4 + (step.n + 1))
                    dve.tensor_tensor_scan(run[:], eq[:], zeros[:], offset[:, ds(b, 1)], ALU.add,
                                           ALU.add).then_inc(chain, 1)
                    dve.wait_ge(chain, b * 4 + (step.n + 2))
                    dve.tensor_tensor(run[:], run[:], eq[:], ALU.mult).then_inc(chain, 1)
                    dve.wait_ge(chain, b * 4 + (step.n + 3))
                    dve.tensor_tensor(pos[:], pos[:], run[:], ALU.add).then_inc(chain, 1)
                    dve.wait_ge(chain, b * 4 + (step.n + 4))
                step.n += 4 * NB
                step(dve.tensor_copy(ints[:], pos[:]))
                step(dve.tensor_scalar(row[o][:], ints[:], P - 1, None, ALU.bitwise_and))
                step(dve.tensor_copy(run[:], row[o][:]))
                step(dve.tensor_scalar(row[o][:], ints[:], 7, None, ALU.logical_shift_right))
                step(dve.tensor_copy(eq[:], row[o][:]))
                dve.scalar_tensor_tensor(out=row[o][:], in0=run[:], scalar=float(CHUNKS), in1=eq[:],
                                         op0=ALU.mult, op1=ALU.add).then_inc(rows_made, 1)
                dve.wait_ge(rows_made, n + 1)


def alloc_constants(nc, ctx):
    shapes = {"ones": [P, P], "iota": [P, P], "ident": [P, P], "before": [P, P], "zeros": [P, P], "gate": [1, 1 + SLOTS]}
    k = {n: ctx.enter_context(nc.sbuf_tensor("c_" + n, s, F32)) for n, s in shapes.items()}
    k["chunk_start"] = ctx.enter_context(nc.sbuf_tensor("c_chunk_start", [P, CHUNKS], I32))
    for o in ("in", "out"):
        k["blk_" + o] = ctx.enter_context(nc.sbuf_tensor("blk_" + o, [1, CHUNKS], I32))
    return k


def block_ids(nc, engine, blks, it, s):
    _, values = nc.values_load_multi_w_load_instructions(
        blks[0:1, ds(it * STEP + s * G, G)], engines=[engine], min_val=0, max_val=NB - 1,
        skip_runtime_bounds_check_because="a chunk's block is a count of at most NB, less one")
    return values


def add_to_blocks(nc, dve, blks, acc, psum, width, it, s, summed, added):
    at = block_ids(nc, DVE, blks, it, s)
    for c, b in enumerate(at):
        if c == 0:
            dve.wait_ge(summed, it + 1)
            if s == 0:
                wait_count(dve, added[SLOTS - 1], it * G)
            else:
                dve.wait_ge(added[s - 1], it * G + G)
        else:
            dve.wait_ge(added[s], it * G + c)
        dst = acc[:, ds(b, 1), 0:width]
        dve.tensor_tensor(dst, dst, psum[:, c:c + 1, 0:width], ALU.add).then_inc(added[s], 1)


def edge_sums(nc, name, k, order, table, gathered, acc, width, first_rec=None):
    with ExitStack() as ctx:
        st = Stage(nc, ctx, name)
        sb, ps, sem, sems = st.sb, st.ps, st.sem, st.sems
        words = XW if first_rec is not None else gathered
        far, low, blks = k["far_" + order], k["low_" + order], k["blk_" + order]
        rowbuf = [sb(f"rows{s}", [P, G, words]) for s in range(SLOTS)]
        hot = [sb(f"hot{s}", [P, G, P]) for s in range(SLOTS)]
        index = [sb(f"index{s}", [P, G], I32) for s in range(SLOTS)]
        pw = 256 if width > P else P
        psum = [ps(f"sum{s}", [P, G, pw]) for s in range(SLOTS)]
        acc_zero = sem("acc_zero")
        rec_in, staged, passed = sems("rec_in"), sems("staged"), sems("passed")
        rows_in = k["dma_" + name]
        hot_made, summed, added = sems("hot_made"), sems("summed"), sems("added")
        block = st.block()

        if first_rec is not None:
            lanes = first_rec.rearrange("(p c) w -> p c w", p=P)

            @block.sync
            def _(sp):
                for it in steps(sp, ITERS):
                    for s in range(SLOTS):
                        wait_count(sp, staged[s], it * 2)
                        wait_count(sp, summed[s], it)
                        sp.dma_start(rowbuf[s][:, :, F:XW], lanes[:, ds(it * STEP + s * G, G), :]).then_inc(rec_in[s], 16)

        @block.scalar
        def _(act):
            for it in steps(act, ITERS):
                for s in range(SLOTS):
                    at = ds(it * STEP + s * G, G)
                    if first_rec is not None:
                        act.wait_ge(passed[s], it + 1)
                        act.wait_ge(rec_in[s], it * 16 + 16)
                        act.copy(far[:, at], rowbuf[s][:, :, 2 * F + 1].bitcast(I32)).then_inc(staged[s], 1)
                        act.copy(low[:, at], rowbuf[s][:, :, 2 * F + 2]).then_inc(staged[s], 1)
                    else:
                        wait_count(act, rows_in[s], it * (16 * G))
                        wait_count(act, passed[s], it)
                        act.copy(index[s][:], far[:, at]).then_inc(staged[s], 1)

        @block.gpsimd
        def _(pool):
            for it in steps(pool, ITERS):
                for s in range(SLOTS):
                    if first_rec is not None:
                        pool.wait_ge(rec_in[s], it * 16 + 16)
                        idx = [rowbuf[s][:, c, 2 * F + 1:2 * F + 2].bitcast(I32) for c in range(G)]
                    else:
                        pool.wait_ge(staged[s], it + 1)
                        wait_count(pool, summed[s], it)
                        idx = [index[s][:, c:c + 1] for c in range(G)]
                    turnstile(pool, k["gate"], s, passed[s])
                    for c in range(G):
                        pool.indirect_dma_start(
                            out=rowbuf[s][:, c, 0:gathered], out_offset=None, in_=table,
                            in_offset=bass.IndirectOffsetOnAxis(ap=idx[c], axis=0)).then_inc(rows_in[s], 16)

        @block.vector
        def _(dve):
            dve.memset(acc[:, :, 0:width], 0.0).then_inc(acc_zero, 1)
            dve.wait_ge(acc_zero, 1)
            for it in steps(dve, ITERS):
                for s in range(SLOTS):
                    wait_count(dve, summed[s], it)
                    if first_rec is not None:
                        dve.wait_ge(rec_in[s], it * 16 + 16)
                        lo = rowbuf[s][:, :, 2 * F + 2]
                    else:
                        lo = low[:, ds(it * STEP + s * G, G)]
                    dve.tensor_tensor(hot[s][:], bc(k["iota"][:], 1, G), bc(lo, 2, P),
                                      ALU.is_equal).then_inc(hot_made[s], 1)
                    add_to_blocks(nc, dve, blks, acc, psum[s], width, it, s, summed[s], added)

        @block.tensor
        def _(pe):
            for it in steps(pe, ITERS):
                for s in range(SLOTS):
                    wait_count(pe, added[s], it * G)
                    pe.wait_ge(hot_made[s], it + 1)
                    pe.wait_ge(rows_in[s], it * (16 * G) + 16 * G)
                    for c in range(G):
                        mm = pe.matmul(psum[s][:, c, 0:width], hot[s][:, c], rowbuf[s][:, c, 0:width],
                                       start=True, stop=True)
                    mm.then_inc(summed[s], 1)


def layer_norm(dve, step, act_ask, act_done, n, t, tmp, stat, out):
    step(dve.tensor_reduce(stat[:, 0], t, AX_X, ALU.add))
    step(dve.tensor_scalar(stat[:, 0], stat[:, 0], 1.0 / F, None, ALU.mult))
    step(dve.tensor_tensor(t, t, bc(stat[:, 0], 2, F), ALU.subtract))
    step(dve.tensor_tensor(tmp, t, t, ALU.mult))
    step(dve.tensor_reduce(stat[:, 1], tmp, AX_X, ALU.add))
    dve.tensor_scalar(stat[:, 1], stat[:, 1], 1.0 / F, EPS, ALU.mult, ALU.add).then_inc(act_ask, 1)
    dve.wait_ge(act_done, n + 1)
    step(dve.reciprocal(stat[:, 3], stat[:, 2]))
    step(dve.tensor_tensor(out, t, bc(stat[:, 3], 2, F), ALU.mult))


def pair(part, j):
    return part[:, j:j + 2].rearrange("p b f -> p (b f)")


def rows_by_block(table):
    return table.rearrange("(b p) f -> p b f", p=P)


def gin_hidden(nc, k, sb_x, acc, y, x, w1, b1, w2, y_tab):
    with ExitStack() as ctx:
        st = Stage(nc, ctx, "hidden")
        sb, ps, sem, sems = st.sb, st.ps, st.sem, st.sems
        W = NODE_B * P
        w1_sb, b1_sb, w2_sb = sb("w1", [F, H]), sb("b1", [H, 1]), sb("w2", [H, F])
        h0, h0t, h1t = sb("h0", [P, NODE_B + 1, F]), sb("h0t", [F, W]), sb("h1t", [H, W])
        p_t = ps("p_t", [P, 1024])
        p_h = ps("p_h", [H, 1024])
        p_y = ps("p_y", [P, NODE_B, F])
        x_zero, loaded, stored = sem("x_zero"), sem("loaded"), sem("stored")
        h0_made, turned, turned_out = sem("h0_made"), sem("turned"), sem("turned_out")
        hidden, relu_made, y_made, y_kept = sem("hidden"), sem("relu_made"), sem("y_made"), sem("y_kept")
        block = st.block()

        @block.sync
        def _(sp):
            sp.wait_ge(x_zero, 1)
            full = NB - 1
            sp.dma_start(sb_x[:, 0:full], x[0:full * P].rearrange("(b p) f -> p b f", p=P)).then_inc(loaded, 16)
            sp.dma_start(sb_x[0:TAIL, full], x[full * P:N]).then_inc(loaded, 16)
            sp.dma_start(w1_sb[:], w1).then_inc(loaded, 16)
            sp.dma_start(b1_sb[:], b1.rearrange("(h o) -> h o", o=1)).then_inc(loaded, 16)
            sp.dma_start(w2_sb[:], w2).then_inc(loaded, 16)
            sp.wait_ge(y_kept, NODE_STEPS)
            sp.dma_start(rows_by_block(y_tab), y[:]).then_inc(stored, 16)
            sp.wait_ge(stored, 16)

        @block.vector
        def _(dve):
            dve.memset(sb_x[:, NB - 1], 0.0).then_inc(x_zero, 1)
            dve.memset(h0[:, NODE_B], 0.0)
            dve.wait_ge(loaded, 80)
            for i in steps(dve, NODE_STEPS):
                at = ds(i * NODE_B, NODE_B)
                wait_count(dve, turned, i)
                dve.tensor_tensor(h0[:, 0:NODE_B], sb_x[:, at], acc[:, at, 0:F], ALU.add).then_inc(h0_made, 1)
                dve.wait_ge(y_made, i + 1)
                dve.tensor_copy(y[:, at], p_y[:]).then_inc(y_kept, 1)

        @block.scalar
        def _(act):
            act.wait_ge(loaded, 80)
            for i in steps(act, NODE_STEPS):
                act.wait_ge(turned, i + 1)
                act.copy(h0t[:], p_t[0:F, 0:W]).then_inc(turned_out, 1)
                act.wait_ge(hidden, i + 1)
                act.activation(h1t[:], p_h[:, 0:W], ACT.Relu, bias=b1_sb[:, 0:1]).then_inc(relu_made, 1)

        @block.tensor
        def _(pe):
            pe.wait_ge(loaded, 80)
            for i in steps(pe, NODE_STEPS):
                pe.wait_ge(h0_made, i + 1)
                for j in range(NODE_B):
                    mm = pe.transpose(p_t[:, j * P:(j + 1) * P], pair(h0, j), k["ident"][:])
                mm.then_inc(turned, 1)
                pe.wait_ge(turned_out, i + 1)
                pe.matmul(p_h[:, 0:512], w1_sb[:], h0t[:, 0:512], start=True, stop=True)
                pe.matmul(p_h[:, 512:W], w1_sb[:], h0t[:, 512:W], start=True, stop=True).then_inc(hidden, 1)
                pe.wait_ge(relu_made, i + 1)
                wait_count(pe, y_kept, i)
                for j in range(NODE_B):
                    mm = pe.matmul(p_y[:, j], h1t[:, j * P:(j + 1) * P], w2_sb[:], start=True, stop=True)
                mm.then_inc(y_made, 1)


def gin_out(nc, k, sb_x, acc, y, t, b2, x_tab):
    with ExitStack() as ctx:
        st = Stage(nc, ctx, "gin")
        sb, ps, sem, sems = st.sb, st.ps, st.sem, st.sems
        b2_sb = sb("b2", [P, F])
        stat = sb("stat", [P, 4, NB])
        loaded = sem("loaded")
        chain = sem("chain")
        ask, root = sem("var_made"), sem("root_made")
        normed = sem("normed")
        stored = sem("stored")
        block = st.block()

        @block.sync
        def _(sp):
            sp.dma_start(b2_sb[:], b2.partition_broadcast(P)).then_inc(loaded, 16)
            sp.wait_ge(normed, 1)
            sp.dma_start(rows_by_block(x_tab), sb_x[:]).then_inc(stored, 16)
            sp.wait_ge(stored, 16)

        @block.scalar
        def _(act):
            act.wait_ge(ask, 1)
            act.activation(stat[:, 2], stat[:, 1], ACT.Sqrt).then_inc(root, 1)

        @block.vector
        def _(dve):
            step = Chain(dve, chain)
            dve.wait_ge(loaded, 16)
            step(dve.tensor_tensor(t[:], sb_x[:], y[:], ALU.add))
            step(dve.tensor_tensor(t[:], t[:], acc[:, :, 0:F], ALU.add))
            step(dve.tensor_tensor(t[:], t[:], bc(b2_sb[:], 1, NB), ALU.add))
            layer_norm(dve, step, ask, root, 0, t[:], y[:], stat, sb_x[:])
            dve.tensor_copy(stat[:, 0], stat[:, 3]).then_inc(normed, 1)


def message_out(nc, k, sb_x, acc, acc_ea, t, tmp, dis, ew1, a_tab, b_tab):
    with ExitStack() as ctx:
        st = Stage(nc, ctx, "message")
        sb, ps, sem, sems = st.sb, st.ps, st.sem, st.sems
        W = NODE_B * P
        w_ab = sb("w_ab", [F, 2, H])
        stat, part, xt = sb("stat", [P, 4, NB]), sb("part", [P, NODE_B + 1, F]), sb("xt", [F, W])
        ab = sb("ab", [P, NODE_B, 2, H])
        p_t = ps("p_t", [P, 1024])
        p_ab = ps("p_ab", [P, 8, 2, H])
        loaded, chain, ask, root = sem("loaded"), sem("chain"), sem("var_made"), sem("root_made")
        staged, turned, turned_out = sem("staged"), sem("turned"), sem("turned_out")
        ab_made, ab_out, stored = sem("ab_made"), sem("ab_out"), sem("stored")
        block = st.block()

        @block.sync
        def _(sp):
            sp.dma_start(w_ab[:], ew1[0:2 * F].rearrange("(s f) h -> f s h", s=2)).then_inc(loaded, 16)
            for i in steps(sp, NODE_STEPS):
                at = ds(i * NODE_B, NODE_B)
                sp.wait_ge(ab_out, i + 1)
                sp.dma_start(rows_by_block(a_tab)[:, at], ab[:, :, 0]).then_inc(stored, 16)
                sp.dma_start(rows_by_block(b_tab)[:, at], ab[:, :, 1]).then_inc(stored, 16)
            sp.wait_ge(stored, 32 * NODE_STEPS)

        @block.scalar
        def _(act):
            for n in range(2):
                act.wait_ge(ask, n + 1)
                act.activation(stat[:, 2], stat[:, 1], ACT.Sqrt).then_inc(root, 1)
            for i in steps(act, NODE_STEPS):
                act.wait_ge(turned, i + 1)
                act.copy(xt[:], p_t[0:F, 0:W]).then_inc(turned_out, 1)
                act.wait_ge(ab_made, i + 1)
                wait_count(act, stored, i * 32)
                act.copy(ab[:], p_ab[:, 0:NODE_B]).then_inc(ab_out, 1)

        @block.vector
        def _(dve):
            step = Chain(dve, chain)
            dve.memset(part[:, NODE_B], 0.0)
            deg = acc_ea[:, :, 2 * F]
            step(dve.tensor_scalar(stat[:, 0], deg, 0.0, None, ALU.is_gt))
            dve.tensor_scalar(stat[:, 1], deg, 1.0, None, ALU.max).then_inc(ask, 1)
            dve.wait_ge(root, 1)
            step(dve.reciprocal(stat[:, 3], stat[:, 2]))
            step(dve.tensor_tensor(dis[:], stat[:, 3], stat[:, 0], ALU.mult))
            step(dve.tensor_tensor(t[:], sb_x[:], bc(deg, 2, F), ALU.mult))
            step(dve.tensor_tensor(t[:], t[:], acc[:, :, 0:F], ALU.add))
            step(dve.tensor_tensor(t[:], t[:], acc_ea[:, :, F:2 * F], ALU.add))
            step(dve.tensor_tensor(t[:], t[:], sb_x[:], ALU.add))
            layer_norm(dve, step, ask, root, 1, t[:], tmp[:], stat, sb_x[:])
            for i in steps(dve, NODE_STEPS):
                wait_count(dve, turned, i)
                dve.tensor_copy(part[:, 0:NODE_B], sb_x[:, ds(i * NODE_B, NODE_B)]).then_inc(staged, 1)

        @block.tensor
        def _(pe):
            pe.wait_ge(loaded, 16)
            for i in steps(pe, NODE_STEPS):
                pe.wait_ge(staged, i + 1)
                for j in range(NODE_B):
                    mm = pe.transpose(p_t[:, j * P:(j + 1) * P], pair(part, j), k["ident"][:])
                mm.then_inc(turned, 1)
                pe.wait_ge(turned_out, i + 1)
                wait_count(pe, ab_out, i)
                for j in range(NODE_B):
                    mm = pe.matmul(p_ab[:, j], xt[:, j * P:(j + 1) * P], w_ab[:], start=True, stop=True)
                mm.then_inc(ab_made, 1)


def edge_mlp(nc, k, out_rec, a_tab, b_tab, acc, ew1, eb1, ew2, eb2):
    with ExitStack() as ctx:
        st = Stage(nc, ctx, "edge_mlp")
        sb, ps, sem, sems = st.sb, st.ps, st.sem, st.sems
        far, low, blks = k["far_out"], k["low_out"], k["blk_out"]
        w_attr, w2_sb = sb("w_attr", [P, G, H]), sb("w2", [H, H])
        b1_sb, b2_row = sb("b1", [H, 1]), sb("b2_row", [1, H])
        b2_rest, b2_part, ones_row = sb("b2_rest", [1, H]), sb("b2_part", [1, 3, H], BF16), sb("ones_row", [1, P], BF16)
        hot_b, ident_b = sb("hot_b", [P, G, P], BF16), sb("ident_b", [P, P], BF16)
        recs = [sb(f"recs{s}", [P, G, OUT_REC]) for s in range(SLOTS)]
        a_blk = [sb(f"a_blk{s}", [P, G, H]) for s in range(SLOTS)]
        b_rows = [sb(f"b_rows{s}", [P, G, H]) for s in range(SLOTS)]
        hot = [sb(f"hot{s}", [P, G, P]) for s in range(SLOTS)]
        hot_t, attr_t = sb("hot_t", [P, G, P]), sb("attr_t", [P, P])
        h, m = sb("h", [H, G, P]), sb("m", [P, G, H])
        p_hot = ctx.enter_context(nc.psum_tensor("edge_mlp_p_hot", [P, 2, G, P], BF16))[:, 0]
        p_attr, p_pre, p_m = ps("p_attr", [P, 512]), ps("p_pre", [H, G, P]), ps("p_m", [P, G, H])
        p_sum = [ps(f"p_sum{q}", [P, G, H]) for q in range(2)]
        set0, loaded, acc_zero = sem("w_attr_zero"), sem("loaded"), sem("acc_zero")
        rec_in, a_in, passed, kept = sems("rec_in"), sems("a_in"), sems("passed"), sems("kept")
        b_in = k["dma_edge_mlp"]
        hot_made, summed, added = sems("hot_made"), sems("summed"), sems("added")
        turned, hot_t_out, attr_t_out = sem("turned"), sem("hot_t_out"), sem("attr_t_out")
        hot_b_made, hot_turned, split = sem("hot_b_made"), sem("hot_turned"), sem("b2_split")
        pre_made, h_made, m_pre, m_made = sem("pre_made"), sem("h_made"), sem("m_pre"), sem("m_made")
        lanes = out_rec.rearrange("(p c) w -> p c w", p=P)
        block = st.block()

        @block.sync
        def _(sp):
            sp.wait_ge(set0, 1)
            for c in range(G):
                sp.dma_start(w_attr[c * OUT_REC:c * OUT_REC + FE + 1, c], ew1[2 * F:2 * F + FE + 1]).then_inc(loaded, 16)
            sp.dma_start(w2_sb[:], ew2).then_inc(loaded, 16)
            sp.dma_start(b1_sb[:], eb1.rearrange("(h o) -> h o", o=1)).then_inc(loaded, 16)
            sp.dma_start(b2_row[:], eb2.rearrange("(o h) -> o h", o=1)).then_inc(loaded, 16)
            for it in steps(sp, ITERS):
                for s in range(SLOTS):
                    wait_count(sp, kept[s], it * 2)
                    wait_count(sp, summed[s], it)
                    sp.dma_start(recs[s][:], lanes[:, ds(it * STEP + s * G, G), :]).then_inc(rec_in[s], 16)
                    for c, b in enumerate(block_ids(nc, SP, blks, it, s)):
                        sp.dma_start(a_blk[s][:, c:c + 1], rows_by_block(a_tab)[:, ds(b, 1)]).then_inc(a_in[s], 16)

        @block.gpsimd
        def _(pool):
            for it in steps(pool, ITERS):
                for s in range(SLOTS):
                    pool.wait_ge(rec_in[s], it * 16 + 16)
                    turnstile(pool, k["gate"], s, passed[s])
                    for c in range(G):
                        pool.indirect_dma_start(
                            out=b_rows[s][:, c], out_offset=None, in_=b_tab,
                            in_offset=bass.IndirectOffsetOnAxis(ap=recs[s][:, c, FE + 1:FE + 2].bitcast(I32), axis=0),
                        ).then_inc(b_in[s], 16)

        def skewed(eng, body):
            for it in steps(eng, ITERS):
                for s in range(SLOTS):
                    body(it, s, s if isinstance(it, int) else SLOTS)

        def before(it, s, by):
            return (it, s - by) if s >= by else (it - 1, s - by + SLOTS)

        @block.tensor
        def _(pe):
            pe.wait_ge(loaded, 16 * (G + 3))
            pe.wait_ge(split, 8)

            def second(it, s):
                pe.wait_ge(h_made, it * SLOTS + s + 1)
                for c in range(G):
                    pe.matmul(p_m[:, c], h[:, c], w2_sb[:], start=True, stop=False)
                    for part in range(3):
                        mm = pe.matmul(p_m[:, c], ones_row[:], b2_part[:, part], start=False, stop=part == 2)
                mm.then_inc(m_pre, 1)

            def total(it, s):
                pe.wait_ge(m_made, it * SLOTS + s + 1)
                q = (s - 2) % SLOTS
                wait_count(pe, added[q], (it * G + G) if s >= 2 else it * G)
                for c in range(G):
                    mm = pe.matmul(p_sum[s % 2][:, c], hot[s][:, c], m[:, c], start=True, stop=True)
                mm.then_inc(summed[s], 1)

            def body(it, s, done):
                pe.wait_ge(rec_in[s], it * 16 + 16)
                pe.wait_ge(hot_made[s], it + 1)
                wait_count(pe, hot_t_out, it * SLOTS + s)
                wait_count(pe, attr_t_out, it * SLOTS + s)
                pe.wait_ge(hot_b_made, it * SLOTS + s + 1)
                for c in range(G):
                    tr = pe.transpose(p_hot[:, c], hot_b[:, c], ident_b[:])
                tr.then_inc(hot_turned, 1)
                pe.transpose(p_attr[:, 0:P], recs[s][:].rearrange("p c w -> p (c w)"), k["ident"][:]).then_inc(turned, 1)
                if done >= 1:
                    second(*before(it, s, 1))
                pe.wait_ge(hot_t_out, it * SLOTS + s + 1)
                pe.wait_ge(attr_t_out, it * SLOTS + s + 1)
                pe.wait_ge(a_in[s], it * (16 * G) + 16 * G)
                pe.wait_ge(b_in[s], it * (16 * G) + 16 * G)
                for c in range(G):
                    pe.matmul(p_pre[:, c], a_blk[s][:, c], hot_t[:, c], start=True, stop=False)
                    pe.matmul(p_pre[:, c], b_rows[s][:, c], k["ident"][:], start=False, stop=False)
                    mm = pe.matmul(p_pre[:, c], w_attr[:, c], attr_t[:], start=False, stop=True)
                mm.then_inc(pre_made, 1)
                if done >= 1:
                    total(*before(it, s, 1))

            skewed(pe, body)
            second(ITERS - 1, SLOTS - 1)
            total(ITERS - 1, SLOTS - 1)

        @block.scalar
        def _(act):
            act.wait_ge(loaded, 16 * (G + 3))

            def message(it, s):
                act.wait_ge(m_pre, it * SLOTS + s + 1)
                wait_count(act, summed[(s - 1) % SLOTS], it if s == 0 else it + 1)
                act.activation(m[:], p_m[:], ACT.Silu).then_inc(m_made, 1)

            def body(it, s, done):
                at = ds(it * STEP + s * G, G)
                act.wait_ge(rec_in[s], it * 16 + 16)
                act.wait_ge(passed[s], it + 1)
                act.copy(far[:, at], recs[s][:, :, FE + 1].bitcast(I32)).then_inc(kept[s], 1)
                act.copy(low[:, at], recs[s][:, :, FE + 2]).then_inc(kept[s], 1)
                act.wait_ge(turned, it * SLOTS + s + 1)
                wait_count(act, pre_made, it * SLOTS + s)
                act.copy(attr_t[:], p_attr[:, 0:P]).then_inc(attr_t_out, 1)
                if done >= 1:
                    message(*before(it, s, 1))
                act.wait_ge(pre_made, it * SLOTS + s + 1)
                act.activation(h[:], p_pre[:], ACT.Silu, bias=b1_sb[:, 0:1]).then_inc(h_made, 1)

            skewed(act, body)
            message(ITERS - 1, SLOTS - 1)

        @block.vector
        def _(dve):
            dve.memset(w_attr[:], 0.0).then_inc(set0, 1)
            dve.memset(ones_row[:], 1.0).then_inc(split, 1)
            dve.tensor_copy(ident_b[:], k["ident"][:]).then_inc(split, 1)
            dve.wait_ge(loaded, 16 * (G + 3))
            rest = [b2_row, b2_rest, b2_rest]
            for part in range(3):
                dve.tensor_copy(b2_part[:, part], rest[part][:]).then_inc(split, 1)
                dve.wait_ge(split, 2 * part + 3)
                dve.tensor_tensor(b2_rest[:], rest[part][:], b2_part[:, part], ALU.subtract).then_inc(split, 1)
                dve.wait_ge(split, 2 * part + 4)
            dve.memset(acc[:, :, 0:H], 0.0).then_inc(acc_zero, 1)
            dve.wait_ge(acc_zero, 1)

            def body(it, s, done):
                dve.wait_ge(rec_in[s], it * 16 + 16)
                dve.tensor_tensor(hot[s][:], bc(k["iota"][:], 1, G), bc(recs[s][:, :, FE + 2], 2, P),
                                  ALU.is_equal).then_inc(hot_made[s], 1)
                wait_count(dve, hot_turned, it * SLOTS + s)
                dve.wait_ge(hot_made[s], it + 1)
                dve.tensor_copy(hot_b[:], hot[s][:]).then_inc(hot_b_made, 1)
                dve.wait_ge(hot_turned, it * SLOTS + s + 1)
                wait_count(dve, pre_made, it * SLOTS + s)
                dve.tensor_copy(hot_t[:], p_hot[:]).then_inc(hot_t_out, 1)
                if done >= 2:
                    pit, q = before(it, s, 2)
                    add_to_blocks(nc, dve, blks, acc, p_sum[q % 2], H, pit, q, summed[q], added)

            skewed(dve, body)
            for q in (SLOTS - 2, SLOTS - 1):
                add_to_blocks(nc, dve, blks, acc, p_sum[q % 2], H, ITERS - 1, q, summed[q], added)


def node_mlp(nc, k, sb_x, acc, t, tmp, dis, z, nw1, nb1, nw2, nb2, z_tab):
    with ExitStack() as ctx:
        st = Stage(nc, ctx, "node_mlp")
        sb, ps, sem, sems = st.sb, st.ps, st.sem, st.sems
        W = NODE_B * P
        w1x, w1a, b1_sb, w2_sb, b2_sb = sb("w1x", [F, H]), sb("w1a", [H, H]), sb("b1", [H, 1]), sb("w2", [H, F]), sb("b2", [P, F])
        stat, x_part, a_part = sb("stat", [P, 4, NB]), sb("x_part", [P, NODE_B + 1, F]), sb("a_part", [P, NODE_B, H])
        xt, at_, ut = sb("xt", [F, W]), sb("at", [H, W]), sb("ut", [H, W])
        p_x = ps("p_x", [P, 1024])
        p_a = ps("p_a", [H, 1024])
        p_u = ps("p_u", [H, 1024])
        p_y = ps("p_y", [P, NODE_B, F])
        loaded, chain, ask, root = sem("loaded"), sem("chain"), sem("var_made"), sem("root_made")
        staged, turned, turned_out, u_made = sem("staged"), sem("turned"), sem("turned_out"), sem("u_made")
        silu_made, y_made, y_kept, z_made, stored = sem("silu_made"), sem("y_made"), sem("y_kept"), sem("z_made"), sem("stored")
        block = st.block()

        @block.sync
        def _(sp):
            sp.dma_start(w1x[:], nw1[0:F]).then_inc(loaded, 16)
            sp.dma_start(w1a[:], nw1[F:F + H]).then_inc(loaded, 16)
            sp.dma_start(b1_sb[:], nb1.rearrange("(h o) -> h o", o=1)).then_inc(loaded, 16)
            sp.dma_start(w2_sb[:], nw2).then_inc(loaded, 16)
            sp.dma_start(b2_sb[:], nb2.partition_broadcast(P)).then_inc(loaded, 16)
            sp.wait_ge(z_made, 2)
            sp.dma_start(rows_by_block(z_tab), z).then_inc(stored, 16)
            sp.wait_ge(stored, 16)

        @block.scalar
        def _(act):
            act.wait_ge(loaded, 80)
            for i in steps(act, NODE_STEPS):
                act.wait_ge(turned, i + 1)
                act.copy(xt[:], p_x[0:F, 0:W]).then_inc(turned_out, 1)
                act.copy(at_[:], p_a[:, 0:W]).then_inc(turned_out, 1)
                act.wait_ge(u_made, i + 1)
                act.activation(ut[:], p_u[:, 0:W], ACT.Silu, bias=b1_sb[:, 0:1]).then_inc(silu_made, 1)
            act.wait_ge(ask, 1)
            act.activation(stat[:, 2], stat[:, 1], ACT.Sqrt).then_inc(root, 1)

        @block.tensor
        def _(pe):
            pe.wait_ge(loaded, 80)
            for i in steps(pe, NODE_STEPS):
                pe.wait_ge(staged, i * 2 + 2)
                for j in range(NODE_B):
                    pe.transpose(p_x[:, j * P:(j + 1) * P], pair(x_part, j), k["ident"][:])
                for j in range(NODE_B):
                    mm = pe.transpose(p_a[:, j * P:(j + 1) * P], a_part[:, j], k["ident"][:])
                mm.then_inc(turned, 1)
                pe.wait_ge(turned_out, i * 2 + 2)
                for lo, hi in ((0, 512), (512, W)):
                    pe.matmul(p_u[:, lo:hi], w1x[:], xt[:, lo:hi], start=True, stop=False)
                    mm = pe.matmul(p_u[:, lo:hi], w1a[:], at_[:, lo:hi], start=False, stop=True)
                mm.then_inc(u_made, 1)
                pe.wait_ge(silu_made, i + 1)
                wait_count(pe, y_kept, i)
                for j in range(NODE_B):
                    mm = pe.matmul(p_y[:, j], ut[:, j * P:(j + 1) * P], w2_sb[:], start=True, stop=True)
                mm.then_inc(y_made, 1)

        @block.vector
        def _(dve):
            step = Chain(dve, chain)
            dve.memset(x_part[:, NODE_B], 0.0)
            dve.wait_ge(loaded, 80)
            for i in steps(dve, NODE_STEPS):
                blocks = ds(i * NODE_B, NODE_B)
                wait_count(dve, turned, i)
                dve.tensor_copy(x_part[:, 0:NODE_B], sb_x[:, blocks]).then_inc(staged, 1)
                dve.tensor_copy(a_part[:], acc[:, blocks, 0:H]).then_inc(staged, 1)
                dve.wait_ge(y_made, i + 1)
                dve.tensor_tensor(t[:, blocks], p_y[:], bc(b2_sb[:], 1, NODE_B), ALU.add).then_inc(y_kept, 1)
            dve.wait_ge(y_kept, NODE_STEPS)
            step(dve.scalar_tensor_tensor(out=t[:], in0=sb_x[:], scalar=2.0, in1=t[:], op0=ALU.mult, op1=ALU.add))
            layer_norm(dve, step, ask, root, 0, t[:], tmp[:], stat, sb_x[:])
            dve.tensor_tensor(z[:, :, 0:F], sb_x[:], bc(dis[:], 2, F), ALU.mult).then_inc(z_made, 1)
            dve.tensor_copy(z[:, :, F], dis[:]).then_inc(z_made, 1)


def filter_out(nc, k, sb_x, acc, t, tmp, dis, w1t, b1, w2t, b2, out):
    with ExitStack() as ctx:
        st = Stage(nc, ctx, "filter")
        sb, ps, sem, sems = st.sb, st.ps, st.sem, st.sems
        W = NODE_B * P
        w, bias, bias2 = sb("w", [2 * F, F]), sb("bias", [P, F]), sb("bias2", [P, F])
        stat, part, pt = sb("stat", [P, 4, NB]), sb("part", [P, NODE_B, 2 * F]), sb("pt", [2 * F, W])
        p_t = ps("p_t", [P, 1024])
        p_y = ps("p_y", [P, NODE_B, F])
        loaded, chain, ask, root = sem("loaded"), sem("chain"), sem("var_made"), sem("root_made")
        staged, turned, turned_out, y_made, y_kept = sem("staged"), sem("turned"), sem("turned_out"), sem("y_made"), sem("y_kept")
        normed, stored = sem("normed"), sem("stored")
        block = st.block()

        @block.sync
        def _(sp):
            sp.dma_start(w[0:F], w1t).then_inc(loaded, 16)
            sp.dma_start(w[F:2 * F], w2t).then_inc(loaded, 16)
            sp.dma_start(bias[:], b1.partition_broadcast(P)).then_inc(loaded, 16)
            sp.dma_start(bias2[:], b2.partition_broadcast(P)).then_inc(loaded, 16)
            sp.wait_ge(normed, 1)
            full = NB - 1
            sp.dma_start(out[0:full * P].rearrange("(b p) f -> p b f", p=P), t[:, 0:full]).then_inc(stored, 16)
            sp.dma_start(out[full * P:N], t[0:TAIL, full]).then_inc(stored, 16)
            sp.wait_ge(stored, 32)

        @block.scalar
        def _(act):
            for i in steps(act, NODE_STEPS):
                act.wait_ge(turned, i + 1)
                act.copy(pt[:], p_t[:, 0:W]).then_inc(turned_out, 1)
            act.wait_ge(ask, 1)
            act.activation(stat[:, 2], stat[:, 1], ACT.Sqrt).then_inc(root, 1)

        @block.tensor
        def _(pe):
            pe.wait_ge(loaded, 64)
            for i in steps(pe, NODE_STEPS):
                pe.wait_ge(staged, i * 2 + 2)
                for j in range(NODE_B):
                    mm = pe.transpose(p_t[:, j * P:(j + 1) * P], part[:, j], k["ident"][:])
                mm.then_inc(turned, 1)
                pe.wait_ge(turned_out, i + 1)
                wait_count(pe, y_kept, i)
                for j in range(NODE_B):
                    mm = pe.matmul(p_y[:, j], pt[:, j * P:(j + 1) * P], w[:], start=True, stop=True)
                mm.then_inc(y_made, 1)

        @block.vector
        def _(dve):
            step = Chain(dve, chain)
            dve.wait_ge(loaded, 64)
            step(dve.tensor_tensor(bias[:], bias[:], bias2[:], ALU.add))
            for i in steps(dve, NODE_STEPS):
                blocks = ds(i * NODE_B, NODE_B)
                wait_count(dve, turned, i)
                dve.tensor_copy(part[:, :, 0:F], acc[:, blocks, 0:F]).then_inc(staged, 1)
                dve.tensor_tensor(part[:, :, F:2 * F], acc[:, blocks, 0:F], sb_x[:, blocks], ALU.mult).then_inc(staged, 1)
                dve.wait_ge(y_made, i + 1)
                dve.tensor_copy(t[:, blocks], p_y[:]).then_inc(y_kept, 1)
            dve.wait_ge(y_kept, NODE_STEPS)
            step(dve.tensor_tensor(tmp[:], bc(bias[:], 1, NB), bc(acc[:, :, F], 2, F), ALU.mult))
            step(dve.tensor_tensor(t[:], t[:], tmp[:], ALU.add))
            step(dve.tensor_tensor(t[:], t[:], bc(dis[:], 2, F), ALU.mult))
            step(dve.scalar_tensor_tensor(out=tmp[:], in0=t[:], scalar=0.2, in1=t[:], op0=ALU.mult, op1=ALU.max))
            step(dve.tensor_tensor(t[:], tmp[:], sb_x[:], ALU.add))
            layer_norm(dve, step, ask, root, 0, t[:], tmp[:], stat, tmp[:])
            dve.tensor_copy(t[:], tmp[:]).then_inc(normed, 1)


def gnn_stack(nc, x, src, dst, ea16, ea64, weight, g_w1, g_b1, g_w2, g_b2, ew1, eb1, ew2, eb2,
              nw1, nb1, nw2, nb2, f_w1t, f_b1, f_w2t, f_b2, out):
    rows = NB * P
    in_rec = nc.dram_tensor("in_records", [P * CHUNKS, IN_REC], F32).ap()
    out_rec = nc.dram_tensor("out_records", [P * CHUNKS, OUT_REC], F32).ap()
    y_tab, x_tab = (nc.dram_tensor(n, [rows, F], F32).ap() for n in ("y_table", "x_table"))
    a_tab, b_tab = (nc.dram_tensor(n, [rows, H], F32).ap() for n in ("a_table", "b_table"))
    z_tab = nc.dram_tensor("z_table", [rows, F + 1], F32).ap()
    with ExitStack() as ctx:
        st = Stage(nc, ctx, "nodes")
        sb, ps, sem, sems = st.sb, st.ps, st.sem, st.sems
        k = alloc_constants(nc, ctx)
        for name in ("scatter", "sum_x", "sum_y", "sum_x1", "edge_mlp", "sum_z"):
            k["dma_" + name] = [ctx.enter_context(nc.semaphore(f"dma_{name}{s}")) for s in range(SLOTS)]
        constants(nc, k)
        sort_edges(nc, k, src, dst, ea16, ea64, weight, in_rec, out_rec)
        for o in ("in", "out"):
            k["far_" + o] = sb("far_" + o, [P, CHUNKS], I32)
            k["low_" + o] = sb("low_" + o, [P, CHUNKS])
        node_x, node_y, node_t = (sb(n, [P, NB, F]) for n in ("node_x", "node_y", "node_t"))
        wide = sb("wide_sums", [P, NB, 2 * F + 1])
        sums = sb("sums", [P, NB, F])
        dis = sb("dis", [P, NB])
        edge_sums(nc, "sum_x", k, "in", x, F, wide, 2 * F + 1, first_rec=in_rec)
        gin_hidden(nc, k, node_x, wide, node_y, x, g_w1, g_b1, g_w2, y_tab)
        edge_sums(nc, "sum_y", k, "in", y_tab, F, sums, F)
        gin_out(nc, k, node_x, sums, node_y, node_t, g_b2, x_tab)
        edge_sums(nc, "sum_x1", k, "in", x_tab, F, sums, F)
        message_out(nc, k, node_x, sums, wide, node_t, node_y, dis, ew1, a_tab, b_tab)
        edge_mlp(nc, k, out_rec, a_tab, b_tab, wide, ew1, eb1, ew2, eb2)
        node_mlp(nc, k, node_x, wide, node_t, node_y, dis, wide[:, :, 0:F + 1], nw1, nb1, nw2, nb2, z_tab)
        edge_sums(nc, "sum_z", k, "out", z_tab, F + 1, wide, F + 1)
        filter_out(nc, k, node_x, wide, node_t, node_y, dis, f_w1t, f_b1, f_w2t, f_b2, out)


NAMES = ["x", "src", "dst", "edge_attr_16", "edge_attr_64", "edge_weight", "L0_gnn_W1", "L0_gnn_b1", "L0_gnn_W2",
         "L0_gnn_b2", "L2_gnn_ew1", "L2_gnn_eb1", "L2_gnn_ew2", "L2_gnn_eb2", "L2_gnn_nw1", "L2_gnn_nb1",
         "L2_gnn_nw2", "L2_gnn_nb2", "L3_gnn_W1", "L3_gnn_b1", "L3_gnn_W2", "L3_gnn_b2"]


def kernel(**inputs):
    import numpy as np
    import concourse.bacc as bacc
    from concourse.bass_utils import run_bass_kernel_spmd

    nc = bacc.Bacc("TRN2", target_bir_lowering=False, num_devices=1)
    arrays, args = {}, []
    for name in NAMES:
        a = np.asarray(inputs[name])
        if name in ("L3_gnn_W1", "L3_gnn_W2"):
            a = a.T
        a = np.ascontiguousarray(a)
        arrays["in_" + name] = a
        args.append(nc.dram_tensor("in_" + name, a.shape, mybir.dt.from_np(a.dtype), kind="ExternalInput").ap())
    out = nc.dram_tensor("out", (N, F), F32, kind="ExternalOutput").ap()
    gnn_stack(nc, *args, out)
    r = run_bass_kernel_spmd(nc, [arrays], core_ids=[0])
    return r.results[0]["out"]
```

```python
from contextlib import ExitStack

import concourse.bass as bass
from concourse import mybir

P = 128
N = 6250
E = 206250
F = 64
H = 128
FE = 16
NB = -(-N // P)
TAIL = N - (NB - 1) * P
EP = 125
EC = E // EP
G = 4
SLOTS = 4
STEP = G * SLOTS
CHUNKS = -(-max((E + NB * (P - 1)) // P, -(-E // P) + NB - 1) // STEP) * STEP
ITERS = CHUNKS // STEP
SC = 15
SITERS = EC // (2 * SC)
IN_REC = F + 2
OUT_REC = 32
EDGE_CHUNKS = -(-E // P)
EPS = 1e-5
CUTOFF = 5.0
NODE_B = 7
NODE_STEPS = NB // NODE_B
PRE = 16

assert EP * EC == E and EC % (2 * SC) == 0 and NB == NODE_B * NODE_STEPS and CHUNKS % PRE == 0

ALU = mybir.AluOpType
ACT = mybir.ActivationFunctionType
AX_X = mybir.AxisListType.X
F32 = mybir.dt.float32
BF16 = mybir.dt.bfloat16
I32 = mybir.dt.int32
DVE = mybir.EngineType.DVE
SP = mybir.EngineType.SP
POOL = mybir.EngineType.Pool
ACTIVATION = mybir.EngineType.Activation
ds = bass.ds


class Chain:

    def __init__(self, eng, sem):
        self.eng, self.sem, self.n = eng, sem, 0

    def __call__(self, ins):
        ins.then_inc(self.sem, 1)
        self.n += 1
        self.eng.wait_ge(self.sem, self.n)


class Stage:

    def __init__(self, nc, ctx, name):
        self.nc, self.ctx, self.name, self.signals = nc, ctx, name, []

    def sb(self, name, shape, dt=F32):
        return self.ctx.enter_context(self.nc.sbuf_tensor(f"{self.name}_{name}", shape, dt))

    def ps(self, name, shape):
        return self.ctx.enter_context(self.nc.psum_tensor(f"{self.name}_{name}", shape, F32))

    def sem(self, name):
        self.signals.append(self.ctx.enter_context(self.nc.semaphore(f"{self.name}_{name}")))
        return self.signals[-1]

    def sems(self, name):
        return [self.sem(f"{name}{s}") for s in range(SLOTS)]

    def block(self):
        self.ctx.callback(self.clear)
        return self.ctx.enter_context(self.nc.Block())

    def clear(self):
        with self.nc.Block() as block:
            @block.gpsimd
            def _(pool):
                for signal in self.signals:
                    pool.sem_clear(signal)


def steps(eng, n):
    yield 0
    with eng.Fori(1, n) as i:
        yield i


def wait_count(eng, sem, count):
    if not isinstance(count, int) or count > 0:
        eng.wait_ge(sem, count)


def turnstile(pool, gate, slot, passed):
    pool.tensor_tensor(gate[0:1, slot + 1:slot + 2], gate[0:1, 0:1], gate[0:1, 0:1], ALU.mult).then_inc(passed, 1)


def bc(ap, dim, n):
    return ap.unsqueeze(dim).to_broadcast([*ap.shape[:dim], n, *ap.shape[dim:]])


def constants(nc, k):
    with ExitStack() as ctx:
        st = Stage(nc, ctx, "constants")
        sb, ps, sem, sems = st.sb, st.ps, st.sem, st.sems
        s_ones = sem("ones_set")
        s_sel = sem("masks_set")
        block = st.block()

        @block.gpsimd
        def _(pool):
            nc.gpsimd.memset(k["ones"][:], 1.0).then_inc(s_ones, 1)
            nc.gpsimd.memset(k["gate"][:], 0.0)
            nc.gpsimd.iota(k["iota"][:], [[1, P]], base=0, channel_multiplier=0,
                           allow_small_or_imprecise_dtypes=True)
            nc.gpsimd.iota(k["node_base"][:], [[-P, NB + 1]], base=0, channel_multiplier=0,
                           allow_small_or_imprecise_dtypes=True)
            pool.wait_ge(s_ones, 1)
            nc.gpsimd.affine_select(out=k["ident"][:], in_=k["ones"][:], compare_op=ALU.is_equal, fill=0.0,
                                    base=0, pattern=[[-1, P]], channel_multiplier=1).then_inc(s_sel, 1)
            nc.gpsimd.affine_select(out=k["before"][:], in_=k["ones"][:], compare_op=ALU.is_gt, fill=0.0,
                                    base=0, pattern=[[1, P]], channel_multiplier=-1).then_inc(s_sel, 1)
            nc.gpsimd.memset(k["zeros"][:], 0.0).then_inc(s_sel, 1)
            pool.wait_ge(s_sel, 3)


class EdgeArrays:

    def __init__(self, nc, ctx):
        def sb(name, shape, dt=F32):
            return ctx.enter_context(nc.sbuf_tensor("edges_" + name, shape, dt))

        self.ends = {"in": sb("dst", [EP, EC], I32), "out": sb("src", [EP, EC], I32)}
        self.weight = sb("weight", [EP, EC])
        self.low_out = sb("low_out", [EP, EC])
        self.blk = {o: sb("blk_" + o, [EP, EC]) for o in self.ends}
        self.ints = sb("ints", [EP, EC], I32)
        self.eq, self.run, self.zeros = sb("eq", [EP, EC]), sb("run", [EP, EC]), sb("zeros", [EP, EC])
        self.pos = sb("pos", [EP, EC])
        self.row = sb("row", [EP, EC], I32)
        self.offset = {o: sb("offset_" + o, [EP, NB]) for o in self.ends}


def position_step(dve, a, order, b, chain, base):
    dve.tensor_scalar(a.eq[:], a.blk[order][:], a.iota[0:EP, ds(b, 1)], None, ALU.is_equal).then_inc(chain, 1)
    dve.wait_ge(chain, b * 4 + (base + 1))
    dve.tensor_tensor_scan(a.run[:], a.eq[:], a.zeros[:], a.offset[order][:, ds(b, 1)], ALU.add, ALU.add).then_inc(chain, 1)
    dve.wait_ge(chain, b * 4 + (base + 2))
    dve.tensor_tensor(a.run[:], a.run[:], a.eq[:], ALU.mult).then_inc(chain, 1)
    dve.wait_ge(chain, b * 4 + (base + 3))
    dve.tensor_tensor(a.pos[:], a.pos[:], a.run[:], ALU.add).then_inc(chain, 1)
    dve.wait_ge(chain, b * 4 + (base + 4))


def count_edges(nc, k, a, src, dst, weight):
    with ExitStack() as ctx:
        st = Stage(nc, ctx, "count")
        sb, ps, sem, sems = st.sb, st.ps, st.sem, st.sems
        below = sb("below", [EP, 2])
        next_first = sb("next_first", [EP, 2], I32)
        count = {o: sb("count_" + o, [EP, NB]) for o in a.ends}
        whole, whole_i = sb("whole", [P, NB]), sb("whole_i", [P, NB], I32)
        upto, first = sb("upto", [P, NB]), sb("first", [P, NB])
        chunk0, chunk1, some = sb("chunk0", [P, NB]), sb("chunk1", [P, NB]), sb("some", [P, NB])
        starts = sb("starts", [P, NB + 1])
        shift = sb("shift", [P, NB + 1])
        starts_col, shift_col = sb("starts_col", [NB + 1, 1]), sb("shift_col", [NB + 1, 1])
        after = sb("after", [NB + 1, CHUNKS])
        number, start_edge = sb("number", [P, CHUNKS], I32), sb("start_edge", [P, CHUNKS], I32)
        item_chunk = sb("item_chunk", [1, CHUNKS])
        p_off = {o: ps("p_off_" + o, [P, 512]) for o in a.ends}
        p_tot = {o: ps("p_tot_" + o, [P, 512]) for o in a.ends}
        p_col = ps("p_col", [P, 512])
        p_row = ps("p_row", [1, 2, 512])
        loaded, numbers_made, chain = sem("loaded"), sem("numbers_made"), sem("chain")
        counted, summed, starts_made, col_made = sem("counted"), sem("summed"), sem("starts_made"), sem("col_made")
        after_made, row_made, row_read = sem("after_made"), sem("row_made"), sem("row_read")
        half = CHUNKS // 4
        block = st.block()

        @block.sync
        def _(sp):
            sp.dma_start(a.ends["in"][:], dst.rearrange("(p c) -> p c", p=EP)).then_inc(loaded, 16)
            sp.dma_start(a.ends["out"][:], src.rearrange("(p c) -> p c", p=EP)).then_inc(loaded, 16)
            sp.dma_start(a.weight[:], weight.rearrange("(p c) -> p c", p=EP)).then_inc(loaded, 16)
            sp.dma_start(next_first[0:EP - 1], dst.rearrange("(p c) -> p c", p=EP)[1:EP, 0:2]).then_inc(loaded, 16)

        @block.gpsimd
        def _(pool):
            nc.gpsimd.iota(number[:], [[1, CHUNKS]], base=0, channel_multiplier=0).then_inc(numbers_made, 1)
            nc.gpsimd.iota(start_edge[:], [[P, CHUNKS]], base=0, channel_multiplier=0).then_inc(numbers_made, 1)

        @block.tensor
        def _(pe):
            for n, o in enumerate(("in", "out")):
                pe.wait_ge(counted, 2 * n + 2)
                pe.matmul(p_off[o][0:EP, 0:NB], k["before"][0:EP, 0:EP], count[o][:], start=True, stop=True)
                if o == "in":
                    pe.matmul(p_tot[o][:, 128:130], k["ones"][0:EP, :], below[:], start=True, stop=True)
                pe.matmul(p_tot[o][:, 0:NB], k["ones"][0:EP, :], count[o][:], start=True, stop=True).then_inc(summed, 1)
            for n in range(2):
                pe.wait_ge(starts_made, n + 1)
                pe.transpose(p_col[0:NB + 1, 0:1], starts[0:1, :], k["ident"][0:1, 0:1])
                pe.transpose(p_col[0:NB + 1, 1:2], shift[0:1, :], k["ident"][0:1, 0:1]).then_inc(col_made, 1)
                pe.wait_ge(after_made, n + 1)
                for q in range(4):
                    if 4 * n + q:
                        pe.wait_ge(row_read, 4 * n + q)
                    part = after[:, q * half:(q + 1) * half]
                    pe.matmul(p_row[:, 0, 0:half], k["ones"][0:NB + 1, 0:1], part, start=True, stop=True)
                    pe.matmul(p_row[:, 1, 0:half], shift_col[:], part, start=True, stop=True).then_inc(row_made, 1)

        @block.vector
        def _(dve):
            step = Chain(dve, chain)
            step(dve.memset(a.zeros[:], 0.0))
            step(dve.memset(a.pos[:], 0.0))
            step(dve.memset(below[:], 0.0))
            step(dve.memset(shift[:], 0.0))
            dve.wait_ge(loaded, 64)
            step(dve.tensor_scalar(a.weight[:], a.weight[:], 1.0 / CUTOFF, None, ALU.mult))
            d = a.ends["in"]
            step(dve.tensor_tensor(a.eq[:, 1:EC], d[:, 1:EC], d[:, 0:EC - 1], ALU.is_lt))
            step(dve.tensor_reduce(below[:, 0:1], a.eq[:, 1:EC], AX_X, ALU.add))
            step(dve.tensor_tensor(below[0:EP - 1, 1:2], next_first[0:EP - 1, 0:1], d[0:EP - 1, EC - 1:EC], ALU.is_lt))
            for n, o in enumerate(("in", "out")):
                step(dve.tensor_scalar(a.ints[:], a.ends[o][:], 7, None, ALU.logical_shift_right))
                dve.tensor_copy(a.blk[o][:], a.ints[:]).then_inc(counted, 1)
                dve.wait_ge(counted, 2 * n + 1)
                for b in steps(dve, NB):
                    dve.tensor_scalar(a.eq[:], a.blk[o][:], k["iota"][0:EP, ds(b, 1)], 0.0, ALU.is_equal, ALU.add,
                                      accum_out=count[o][:, ds(b, 1)]).then_inc(chain, 1)
                    dve.wait_ge(chain, b + (step.n + 1))
                step.n += NB
                dve.memset(a.eq[:, 0:1], 0.0).then_inc(counted, 1)
                dve.wait_ge(counted, 2 * n + 2)
            step(dve.tensor_scalar(a.ints[:], a.ends["out"][:], P - 1, None, ALU.bitwise_and))
            step(dve.tensor_copy(a.low_out[:], a.ints[:]))
            dve.wait_ge(summed, 2)
            dve.wait_ge(numbers_made, 2)

            total = p_tot["in"][:, 0:NB]
            step(dve.tensor_reduce(some[:, 0:1], p_tot["in"][:, 128:130], AX_X, ALU.add))
            step(dve.tensor_copy(k["unsorted"][:], some[0:1, 0:1]))
            step(dve.tensor_copy(whole[:], total))
            step(dve.tensor_tensor_scan(upto[:], whole[:], k["zeros"][:, 0:NB], 0.0, ALU.add, ALU.add))
            step(dve.tensor_tensor(first[:], upto[:], whole[:], ALU.subtract))
            step(dve.scalar_tensor_tensor(out=a.offset["in"][:], in0=p_off["in"][0:EP, 0:NB], scalar=-1.0,
                                          in1=first[0:EP, :], op0=ALU.add, op1=ALU.add))
            step(dve.tensor_copy(whole_i[:], first[:]))
            step(dve.tensor_scalar(whole_i[:], whole_i[:], 7, None, ALU.logical_shift_right))
            step(dve.tensor_copy(chunk0[:], whole_i[:]))
            step(dve.tensor_scalar(whole_i[:], upto[:], -1.0, 0.0, ALU.add, ALU.max))
            step(dve.tensor_scalar(whole_i[:], whole_i[:], 7, None, ALU.logical_shift_right))
            step(dve.tensor_copy(chunk1[:], whole_i[:]))
            step(dve.tensor_scalar(some[:], whole[:], 0.0, None, ALU.is_gt))
            step(dve.scalar_tensor_tensor(out=chunk1[:], in0=chunk1[:], scalar=1.0, in1=chunk0[:],
                                          op0=ALU.add, op1=ALU.subtract))
            step(dve.tensor_tensor(chunk1[:], chunk1[:], some[:], ALU.mult))
            step(dve.tensor_tensor_scan(upto[:], chunk1[:], k["zeros"][:, 0:NB], 0.0, ALU.add, ALU.add))
            step(dve.tensor_tensor(starts[:, 0:NB], upto[:], chunk1[:], ALU.subtract))
            step(dve.tensor_copy(starts[:, NB:NB + 1], upto[:, NB - 1:NB]))
            step(dve.tensor_tensor(chunk0[:], chunk0[:], starts[:, 0:NB], ALU.subtract))
            step(dve.tensor_copy(shift[:, 0:1], chunk0[:, 0:1]))
            dve.tensor_tensor(shift[:, 1:NB], chunk0[:, 1:NB], chunk0[:, 0:NB - 1], ALU.subtract).then_inc(starts_made, 1)
            dve.wait_ge(starts_made, 1)

            def rows(n, numbers):
                dve.wait_ge(col_made, n + 1)
                step(dve.tensor_copy(starts_col[:], p_col[0:NB + 1, 0:1]))
                step(dve.tensor_copy(shift_col[:], p_col[0:NB + 1, 1:2]))
                dve.tensor_scalar(after[:], numbers[0:NB + 1, :], starts_col[:, 0:1], None, ALU.is_ge).then_inc(after_made, 1)
                for q in range(4):
                    at = slice(q * half, (q + 1) * half)
                    dve.wait_ge(row_made, 4 * n + q + 1)
                    step(dve.tensor_scalar(k["blk_" + ("in", "out")[n]][:, at], p_row[:, 0, 0:half], -1.0, None, ALU.add))
                    dve.tensor_copy(item_chunk[:, at], p_row[:, 1, 0:half]).then_inc(row_read, 1)
                    dve.wait_ge(row_read, 4 * n + q + 1)

            rows(0, number)
            step(dve.tensor_tensor(item_chunk[:], item_chunk[:], number[0:1, :], ALU.add))
            step(dve.tensor_scalar(k["chunk_in"][:], item_chunk[:], float(EDGE_CHUNKS - 1), None, ALU.min))
            step(dve.tensor_scalar(k["edge_in"][:], item_chunk[:], float(P), float(E - P), ALU.mult, ALU.min))

            step(dve.tensor_scalar(whole_i[:], p_tot["out"][:, 0:NB], float(P - 1), None, ALU.add))
            step(dve.tensor_scalar(whole_i[:], whole_i[:], 7, 7, ALU.logical_shift_right, ALU.arith_shift_left))
            step(dve.tensor_copy(whole[:], whole_i[:]))
            step(dve.tensor_tensor_scan(upto[:], whole[:], k["zeros"][:, 0:NB], 0.0, ALU.add, ALU.add))
            step(dve.tensor_tensor(first[:], upto[:], whole[:], ALU.subtract))
            step(dve.scalar_tensor_tensor(out=a.offset["out"][:], in0=p_off["out"][0:EP, 0:NB], scalar=-1.0,
                                          in1=first[0:EP, :], op0=ALU.add, op1=ALU.add))
            step(dve.tensor_copy(starts[:, 0:NB], first[:]))
            dve.memset(starts[:, NB:NB + 1], float(P * CHUNKS)).then_inc(starts_made, 1)
            dve.wait_ge(starts_made, 2)
            rows(1, start_edge)


def only_if_unsorted(nc, k, eng, engine):
    flag = nc.values_load(k["unsorted"][0:1, 0:1], engines=[engine], min_val=0, max_val=E,
                          skip_runtime_bounds_check_because="a count of edges")
    return eng.If(flag > 0)


def sort_in(nc, k, a, ea64, in_rec):
    with ExitStack() as ctx:
        st = Stage(nc, ctx, "sort_in")
        sb, ps, sem, sems = st.sb, st.ps, st.sem, st.sems
        recs = [sb(f"recs{s}", [EP, SC, IN_REC]) for s in range(2)]
        rows = [sb(f"rows{s}", [EP, SC], I32) for s in range(2)]
        chain, rows_made = sem("chain"), sem("rows_made")
        attr_in, staged, passed = sems("attr_in"), sems("staged"), sems("passed")
        scattered = k["dma_scatter"][0:2]
        attrs = ea64.rearrange("(p c) w -> p c w", p=EP)
        block = st.block()

        @block.sync
        def _(sp):
            with only_if_unsorted(nc, k, sp, SP):
                for i in steps(sp, SITERS):
                    for s in range(2):
                        wait_count(sp, scattered[s], i * (16 * SC))
                        sp.dma_start(recs[s][:, :, 0:F], attrs[:, ds(i * (2 * SC) + s * SC, SC)]).then_inc(attr_in[s], 16)

        @block.gpsimd
        def _(pool):
            with only_if_unsorted(nc, k, pool, POOL):
                for i in steps(pool, SITERS):
                    for s in range(2):
                        pool.wait_ge(attr_in[s], i * 16 + 16)
                        pool.wait_ge(staged[s], i * 3 + 3)
                        turnstile(pool, k["gate"], s, passed[s])
                        for c in range(SC):
                            pool.indirect_dma_start(
                                out=in_rec, out_offset=bass.IndirectOffsetOnAxis(ap=rows[s][:, c:c + 1], axis=0),
                                in_=recs[s][:, c], in_offset=None).then_inc(scattered[s], 16)
                for s in range(2):
                    pool.wait_ge(scattered[s], SITERS * 16 * SC)

        @block.scalar
        def _(act):
            with only_if_unsorted(nc, k, act, ACTIVATION):
                act.wait_ge(rows_made, 1)
                for i in steps(act, SITERS):
                    for s in range(2):
                        wait_count(act, scattered[s], i * (16 * SC))
                        wait_count(act, passed[s], i)
                        at = ds(i * (2 * SC) + s * SC, SC)
                        act.copy(recs[s][:, :, F].bitcast(I32), a.ends["out"][:, at]).then_inc(staged[s], 1)
                        act.copy(recs[s][:, :, F + 1].bitcast(I32), a.ends["in"][:, at]).then_inc(staged[s], 1)
                        act.copy(rows[s][:], a.row[:, at]).then_inc(staged[s], 1)

        @block.vector
        def _(dve):
            with only_if_unsorted(nc, k, dve, DVE):
                for b in steps(dve, NB):
                    position_step(dve, a, "in", b, chain, 0)
                dve.tensor_copy(a.row[:], a.pos[:]).then_inc(rows_made, 1)
                dve.wait_ge(rows_made, 1)
                dve.memset(a.pos[:], 0.0).then_inc(chain, 1)
                dve.wait_ge(chain, 4 * NB + 1)


def tables_in(nc, k, src, dst, in_rec):
    with ExitStack() as ctx:
        st = Stage(nc, ctx, "tables")
        sb, ps, sem, sems = st.sb, st.ps, st.sem, st.sems
        tiles = -(-EDGE_CHUNKS // P)
        full = (tiles - 1) * P
        rest = EDGE_CHUNKS - 1 - full
        rows = {o: sb("rows_" + o, [P, tiles, P], I32) for o in ("far", "near")}
        vals = {o: sb("vals_" + o, [P, tiles, P]) for o in ("far", "near")}
        p_t = [ps(f"p_t{q}", [P, 4, P]) for q in range(2)]
        cleared, loaded, made, turned, kept, cut = (sem("cleared"), sem("loaded"), sem("made"), sem("turned"),
                                                    sem("kept"), sem("cut"))
        groups = [(o, q) for o in ("far", "near") for q in range(0, tiles, 4)]
        block = st.block()

        def load(sp, edge_values, slow):
            for o, ap in edge_values:
                for q in range(tiles - 1):
                    head = ap[q * P * P:(q + 1) * P * P].rearrange("(p e) -> p e", e=P)
                    sp.dma_start(rows[o][:, q], head, allow_slow_non_contiguous=slow).then_inc(loaded, 16)
                body = ap[full * P:(full + rest) * P].rearrange("(p e) -> p e", e=P)
                sp.dma_start(rows[o][0:rest, tiles - 1], body, allow_slow_non_contiguous=slow).then_inc(loaded, 16)
                sp.dma_start(rows[o][rest:rest + 1, tiles - 1], ap[E - P:E].rearrange("(p e) -> p e", e=P),
                             allow_slow_non_contiguous=slow).then_inc(loaded, 16)

        @block.sync
        def _(sp):
            sp.wait_ge(cleared, 2)
            flag = nc.values_load(k["unsorted"][0:1, 0:1], engines=[SP], min_val=0, max_val=E,
                                  skip_runtime_bounds_check_because="a count of edges")
            with sp.If(flag > 0):
                load(sp, (("far", in_rec[:, F].bitcast(I32)), ("near", in_rec[:, F + 1].bitcast(I32))), True)
            with sp.Else():
                load(sp, (("far", src), ("near", dst)), False)

        @block.gpsimd
        def _(pool):
            nc.gpsimd.memset(rows["far"][:, tiles - 1], 0).then_inc(cleared, 1)
            nc.gpsimd.memset(rows["near"][:, tiles - 1], 0).then_inc(cleared, 1)
            pool.wait_ge(kept, len(groups))
            last = k["chunk_near"][:, EDGE_CHUNKS - 1:EDGE_CHUNKS]
            nc.gpsimd.affine_select(out=last, in_=last, compare_op=ALU.is_ge, fill=-1.0, base=E - P * EDGE_CHUNKS,
                                    pattern=[[0, 1]], channel_multiplier=1).then_inc(cut, 1)
            pool.wait_ge(cut, 1)

        @block.vector
        def _(dve):
            dve.wait_ge(loaded, 2 * 16 * (tiles + 1))
            dve.tensor_copy(vals["far"][:], rows["far"][:]).then_inc(made, 1)
            dve.tensor_copy(vals["near"][:], rows["near"][:]).then_inc(made, 1)
            for n, (o, q) in enumerate(groups):
                w = min(4, tiles - q)
                dve.wait_ge(turned, n + 1)
                dest = k["chunk_" + o][:, q * P:(q + w) * P].rearrange("p (c e) -> p c e", e=P)
                dve.tensor_copy(dest, p_t[n % 2][:, 0:w]).then_inc(kept, 1)

        @block.tensor
        def _(pe):
            pe.wait_ge(made, 2)
            for n, (o, q) in enumerate(groups):
                if n >= 2:
                    pe.wait_ge(kept, n - 1)
                for j in range(min(4, tiles - q)):
                    mm = pe.transpose(p_t[n % 2][:, j], vals[o][:, q + j], k["ident"][:])
                mm.then_inc(turned, 1)


def scatter_out(nc, k, a, ea16, out_rec):
    with ExitStack() as ctx:
        st = Stage(nc, ctx, "scatter_out")
        sb, ps, sem, sems = st.sb, st.ps, st.sem, st.sems
        recs = [sb(f"recs{s}", [EP, SC, OUT_REC]) for s in range(2)]
        rows = [sb(f"rows{s}", [EP, SC], I32) for s in range(2)]
        cleared = sem("cleared")
        attr_in, staged, passed = sems("attr_in"), sems("staged"), sems("passed")
        scattered = k["dma_scatter"][2:4]
        attrs = ea16.rearrange("(p c) w -> p c w", p=EP)
        block = st.block()

        @block.sync
        def _(sp):
            sp.wait_ge(cleared, 2)
            for i in steps(sp, SITERS):
                for s in range(2):
                    wait_count(sp, scattered[s], i * (16 * SC))
                    sp.dma_start(recs[s][:, :, 0:FE], attrs[:, ds(i * (2 * SC) + s * SC, SC)]).then_inc(attr_in[s], 16)

        @block.vector
        def _(dve):
            for s in range(2):
                dve.memset(recs[s][:], 0.0).then_inc(cleared, 1)

        @block.gpsimd
        def _(pool):
            for i in steps(pool, SITERS):
                for s in range(2):
                    pool.wait_ge(attr_in[s], i * 16 + 16)
                    pool.wait_ge(staged[s], i * 4 + 4)
                    turnstile(pool, k["gate"], s, passed[s])
                    for c in range(SC):
                        pool.indirect_dma_start(
                            out=out_rec, out_offset=bass.IndirectOffsetOnAxis(ap=rows[s][:, c:c + 1], axis=0),
                            in_=recs[s][:, c], in_offset=None).then_inc(scattered[s], 16)
            for s in range(2):
                pool.wait_ge(scattered[s], SITERS * 16 * SC)

        @block.scalar
        def _(act):
            act.wait_ge(cleared, 2)
            for i in steps(act, SITERS):
                for s in range(2):
                    wait_count(act, scattered[s], i * (16 * SC))
                    wait_count(act, passed[s], i)
                    at = ds(i * (2 * SC) + s * SC, SC)
                    act.copy(recs[s][:, :, FE], a.weight[:, at]).then_inc(staged[s], 1)
                    act.copy(recs[s][:, :, FE + 1].bitcast(I32), a.ends["in"][:, at]).then_inc(staged[s], 1)
                    act.copy(recs[s][:, :, FE + 2], a.low_out[:, at]).then_inc(staged[s], 1)
                    act.copy(rows[s][:], a.row[:, at]).then_inc(staged[s], 1)


def alloc_constants(nc, ctx):
    shapes = {"ones": [P, P], "iota": [P, P], "ident": [P, P], "before": [P, P], "zeros": [P, P], "gate": [1, 1 + SLOTS],
              "node_base": [P, NB + 1]}
    k = {n: ctx.enter_context(nc.sbuf_tensor("c_" + n, s, F32)) for n, s in shapes.items()}
    for n, w in (("blk_in", CHUNKS), ("blk_out", CHUNKS), ("chunk_in", CHUNKS), ("edge_in", CHUNKS), ("unsorted", 1)):
        k[n] = ctx.enter_context(nc.sbuf_tensor(n, [1, w], I32))
    tiles = -(-EDGE_CHUNKS // P)
    for n, w, dt in (("chunk_far", tiles * P, I32), ("chunk_near", tiles * P, F32), ("far_in", CHUNKS, I32),
                     ("low_in", CHUNKS, F32)):
        k[n] = ctx.enter_context(nc.sbuf_tensor(n, [P, w], dt))
    return k


def load_row(nc, engine, row, it, s, top, why, late=0):
    _, values = nc.values_load_multi_w_load_instructions(
        row[0:1, ds(it * STEP + (s * G - late * STEP), G)], engines=[engine], min_val=0, max_val=top,
        skip_runtime_bounds_check_because=why)
    return values


def block_ids(nc, engine, blks, it, s, top=NB - 1, late=0):
    return load_row(nc, engine, blks, it, s, top, "how many of the blocks have begun, less one", late)


def item_chunks(nc, engine, k, it, s):
    return load_row(nc, engine, k["chunk_in"], it, s, EDGE_CHUNKS - 1, "clamped to the last chunk")


def item_edges(nc, engine, k, it, s):
    return load_row(nc, engine, k["edge_in"], it, s, E - P, "clamped to the last chunk's first edge")


def add_to_blocks(nc, dve, at, acc, psum, width, it, s, summed, added, late=0):
    for c, b in enumerate(at):
        if c == 0:
            dve.wait_ge(summed, it + (1 - late))
            if s == 0:
                wait_count(dve, added[SLOTS - 1], it * G)
            else:
                dve.wait_ge(added[s - 1], it * G + G * (1 - late))
        else:
            dve.wait_ge(added[s], it * G + (c - G * late))
        dst = acc[:, ds(b, 1), 0:width]
        dve.tensor_tensor(dst, dst, psum[:, c:c + 1, 0:width], ALU.add).then_inc(added[s], 1)


def edge_sums(nc, name, k, order, table, gathered, acc, width, attrs=None, a=None, out_rec=None):
    with ExitStack() as ctx:
        st = Stage(nc, ctx, name)
        sb, ps, sem, sems = st.sb, st.ps, st.sem, st.sems
        first = attrs is not None
        far, low, blks = k["far_" + order], k["low_" + order], k["blk_" + order]
        rowbuf = [sb(f"rows{s}", [P, G, 2 * F + 1 if first else gathered]) for s in range(SLOTS)]
        hot = [sb(f"hot{s}", [P, G, P]) for s in range(SLOTS)]
        index = [sb(f"index{s}", [P, G], I32) for s in range(SLOTS)]
        pw = 256 if width > P else P
        psum = [ps(f"sum{s}", [P, G, pw]) for s in range(SLOTS)]
        acc_zero, ones_set, pad_set, prefilled = sem("acc_zero"), sem("ones_set"), sem("pad_set"), sem("prefilled")
        attr_in, staged, passed = sems("attr_in"), sems("staged"), sems("passed")
        rows_in = k["dma_" + name]
        listed = sems("listed") if first else None
        hot_made, summed, added, chain = sems("hot_made"), sems("summed"), sems("added"), sem("chain")
        if first:
            padding = sb("padding", [P, PRE, OUT_REC])
        block = st.block()

        if first:
            @block.sync
            def _(sp):
                def load(source):
                    for it in steps(sp, ITERS):
                        for s in range(SLOTS):
                            edges = item_edges(nc, SP, k, it, s)
                            wait_count(sp, summed[s], it)
                            for c, e in enumerate(edges):
                                sp.dma_start(rowbuf[s][:, c, F:2 * F], source[ds(e, P), 0:F]).then_inc(attr_in[s], 16)

                flag = nc.values_load(k["unsorted"][0:1, 0:1], engines=[SP], min_val=0, max_val=E,
                                      skip_runtime_bounds_check_because="a count of edges")
                with sp.If(flag > 0):
                    load(attrs[1])
                with sp.Else():
                    load(attrs[0])

        @block.scalar
        def _(act):
            if first:
                act.wait_ge(pad_set, 2)
                lanes = out_rec.rearrange("(p c) w -> p c w", p=P)
                for i in steps(act, CHUNKS // PRE):
                    act.dma_start(lanes[:, ds(i * PRE, PRE)], padding[:]).then_inc(prefilled, 16)
            for it in steps(act, ITERS):
                for s in range(SLOTS):
                    wait_count(act, rows_in[s], it * (16 * G))
                    wait_count(act, passed[s], it)
                    if first:
                        ids = block_ids(nc, ACTIVATION, blks, it, s, NB)
                        chunks = item_chunks(nc, ACTIVATION, k, it, s)
                        for c in range(G):
                            item = ds(it * STEP + (s * G + c), 1)
                            chunk = ds(chunks[c], 1)
                            act.copy(index[s][:, c:c + 1], k["chunk_far"][:, chunk]).then_inc(staged[s], 1)
                            act.copy(far[:, item], k["chunk_far"][:, chunk])
                            act.activation(low[:, item], k["chunk_near"][:, chunk], ACT.Identity,
                                           bias=k["node_base"][:, ds(ids[c], 1)]).then_inc(listed[s], 1)
                    else:
                        act.copy(index[s][:], far[:, ds(it * STEP + s * G, G)]).then_inc(staged[s], 1)
            if first:
                act.wait_ge(prefilled, 16 * (CHUNKS // PRE))

        @block.gpsimd
        def _(pool):
            if first:
                nc.gpsimd.memset(padding[:], 0.0).then_inc(pad_set, 1)
                pool.wait_ge(pad_set, 1)
                nc.gpsimd.memset(padding[:, :, FE + 2:FE + 3], -1.0).then_inc(pad_set, 1)
            for it in steps(pool, ITERS):
                for s in range(SLOTS):
                    if first:
                        pool.wait_ge(staged[s], it * G + G)
                    else:
                        pool.wait_ge(staged[s], it + 1)
                    wait_count(pool, summed[s], it)
                    turnstile(pool, k["gate"], s, passed[s])
                    for c in range(G):
                        pool.indirect_dma_start(
                            out=rowbuf[s][:, c, 0:gathered], out_offset=None, in_=table,
                            in_offset=bass.IndirectOffsetOnAxis(ap=index[s][:, c:c + 1], axis=0)).then_inc(rows_in[s], 16)

        @block.vector
        def _(dve):
            dve.memset(acc[:, :, 0:width], 0.0).then_inc(acc_zero, 1)
            if first:
                for s in range(SLOTS):
                    dve.memset(rowbuf[s][:, :, 2 * F:2 * F + 1], 1.0).then_inc(ones_set, 1)
            dve.wait_ge(acc_zero, 1)

            def make_hot(it, s):
                wait_count(dve, summed[s], it)
                if first:
                    dve.wait_ge(listed[s], it * G + G)
                lo = low[:, ds(it * STEP + s * G, G)]
                dve.tensor_tensor(hot[s][:], bc(k["iota"][:], 1, G), bc(lo, 2, P), ALU.is_equal).then_inc(hot_made[s], 1)

            def add(it, s, late=0):
                ids = block_ids(nc, DVE, blks, it, s, NB if order == "in" else NB - 1, late)
                add_to_blocks(nc, dve, ids, acc, psum[s], width, it, s, summed[s], added, late)

            def iteration(it):
                for s in range(SLOTS):
                    make_hot(it, s)
                    if s:
                        add(it, s - 1)
                    elif not isinstance(it, int):
                        add(it, SLOTS - 1, 1)

            if first:
                iteration(0)
                position_step(dve, a, "out", 0, chain, 0)
                with dve.Fori(1, NB) as it:
                    iteration(it)
                    position_step(dve, a, "out", it, chain, 0)
                with dve.Fori(NB, ITERS) as it:
                    iteration(it)
                step = Chain(dve, chain)
                step.n = 4 * NB
                step(dve.tensor_copy(a.ints[:], a.pos[:]))
                step(dve.tensor_scalar(a.row[:], a.ints[:], P - 1, None, ALU.bitwise_and))
                step(dve.tensor_copy(a.run[:], a.row[:]))
                step(dve.tensor_scalar(a.row[:], a.ints[:], 7, None, ALU.logical_shift_right))
                step(dve.tensor_copy(a.eq[:], a.row[:]))
                step(dve.scalar_tensor_tensor(out=a.row[:], in0=a.run[:], scalar=float(CHUNKS), in1=a.eq[:],
                                              op0=ALU.mult, op1=ALU.add))
            else:
                for it in steps(dve, ITERS):
                    iteration(it)
            add(ITERS - 1, SLOTS - 1)

        @block.tensor
        def _(pe):
            if first:
                pe.wait_ge(ones_set, SLOTS)
            for it in steps(pe, ITERS):
                for s in range(SLOTS):
                    wait_count(pe, added[s], it * G)
                    pe.wait_ge(hot_made[s], it + 1)
                    if first:
                        pe.wait_ge(attr_in[s], it * (16 * G) + 16 * G)
                    pe.wait_ge(rows_in[s], it * (16 * G) + 16 * G)
                    for c in range(G):
                        mm = pe.matmul(psum[s][:, c, 0:width], hot[s][:, c], rowbuf[s][:, c, 0:width],
                                       start=True, stop=True)
                    mm.then_inc(summed[s], 1)


def layer_norm(dve, step, act_ask, act_done, n, t, tmp, stat, out):
    step(dve.tensor_reduce(stat[:, 0], t, AX_X, ALU.add))
    step(dve.tensor_scalar(stat[:, 0], stat[:, 0], 1.0 / F, None, ALU.mult))
    step(dve.tensor_tensor(t, t, bc(stat[:, 0], 2, F), ALU.subtract))
    step(dve.tensor_tensor(tmp, t, t, ALU.mult))
    step(dve.tensor_reduce(stat[:, 1], tmp, AX_X, ALU.add))
    dve.tensor_scalar(stat[:, 1], stat[:, 1], 1.0 / F, EPS, ALU.mult, ALU.add).then_inc(act_ask, 1)
    dve.wait_ge(act_done, n + 1)
    step(dve.reciprocal(stat[:, 3], stat[:, 2]))
    step(dve.tensor_tensor(out, t, bc(stat[:, 3], 2, F), ALU.mult))


def pair(part, j):
    return part[:, j:j + 2].rearrange("p b f -> p (b f)")


def rows_by_block(table):
    return table.rearrange("(b p) f -> p b f", p=P)


def gin_hidden(nc, k, sb_x, acc, y, x, w1, b1, w2, y_tab):
    with ExitStack() as ctx:
        st = Stage(nc, ctx, "hidden")
        sb, ps, sem, sems = st.sb, st.ps, st.sem, st.sems
        W = NODE_B * P
        w1_sb, b1_sb, w2_sb = sb("w1", [F, H]), sb("b1", [H, 1]), sb("w2", [H, F])
        h0, h0t, h1t = sb("h0", [P, NODE_B + 1, F]), sb("h0t", [F, W]), sb("h1t", [H, W])
        p_t = ps("p_t", [P, 1024])
        p_h = ps("p_h", [H, 1024])
        p_y = ps("p_y", [P, NODE_B, F])
        x_zero, loaded, stored = sem("x_zero"), sem("loaded"), sem("stored")
        h0_made, turned, turned_out = sem("h0_made"), sem("turned"), sem("turned_out")
        hidden, relu_made, y_made, y_kept = sem("hidden"), sem("relu_made"), sem("y_made"), sem("y_kept")
        block = st.block()

        @block.sync
        def _(sp):
            sp.wait_ge(x_zero, 1)
            full = NB - 1
            sp.dma_start(sb_x[:, 0:full], x[0:full * P].rearrange("(b p) f -> p b f", p=P)).then_inc(loaded, 16)
            sp.dma_start(sb_x[0:TAIL, full], x[full * P:N]).then_inc(loaded, 16)
            sp.dma_start(w1_sb[:], w1).then_inc(loaded, 16)
            sp.dma_start(b1_sb[:], b1.rearrange("(h o) -> h o", o=1)).then_inc(loaded, 16)
            sp.dma_start(w2_sb[:], w2).then_inc(loaded, 16)
            sp.wait_ge(y_kept, NODE_STEPS)
            sp.dma_start(rows_by_block(y_tab), y[:]).then_inc(stored, 16)
            sp.wait_ge(stored, 16)

        @block.vector
        def _(dve):
            dve.memset(sb_x[:, NB - 1], 0.0).then_inc(x_zero, 1)
            dve.memset(h0[:, NODE_B], 0.0)
            dve.wait_ge(loaded, 80)
            for i in steps(dve, NODE_STEPS):
                at = ds(i * NODE_B, NODE_B)
                wait_count(dve, turned, i)
                dve.tensor_tensor(h0[:, 0:NODE_B], sb_x[:, at], acc[:, at, 0:F], ALU.add).then_inc(h0_made, 1)
                dve.wait_ge(y_made, i + 1)
                dve.tensor_copy(y[:, at], p_y[:]).then_inc(y_kept, 1)

        @block.scalar
        def _(act):
            act.wait_ge(loaded, 80)
            for i in steps(act, NODE_STEPS):
                act.wait_ge(turned, i + 1)
                act.copy(h0t[:], p_t[0:F, 0:W]).then_inc(turned_out, 1)
                act.wait_ge(hidden, i + 1)
                act.activation(h1t[:], p_h[:, 0:W], ACT.Relu, bias=b1_sb[:, 0:1]).then_inc(relu_made, 1)

        @block.tensor
        def _(pe):
            pe.wait_ge(loaded, 80)
            for i in steps(pe, NODE_STEPS):
                pe.wait_ge(h0_made, i + 1)
                for j in range(NODE_B):
                    mm = pe.transpose(p_t[:, j * P:(j + 1) * P], pair(h0, j), k["ident"][:])
                mm.then_inc(turned, 1)
                pe.wait_ge(turned_out, i + 1)
                pe.matmul(p_h[:, 0:512], w1_sb[:], h0t[:, 0:512], start=True, stop=True)
                pe.matmul(p_h[:, 512:W], w1_sb[:], h0t[:, 512:W], start=True, stop=True).then_inc(hidden, 1)
                pe.wait_ge(relu_made, i + 1)
                wait_count(pe, y_kept, i)
                for j in range(NODE_B):
                    mm = pe.matmul(p_y[:, j], h1t[:, j * P:(j + 1) * P], w2_sb[:], start=True, stop=True)
                mm.then_inc(y_made, 1)


def gin_out(nc, k, sb_x, acc, y, t, b2, x_tab):
    with ExitStack() as ctx:
        st = Stage(nc, ctx, "gin")
        sb, ps, sem, sems = st.sb, st.ps, st.sem, st.sems
        b2_sb = sb("b2", [P, F])
        stat = sb("stat", [P, 4, NB])
        loaded = sem("loaded")
        chain = sem("chain")
        ask, root = sem("var_made"), sem("root_made")
        normed = sem("normed")
        stored = sem("stored")
        block = st.block()

        @block.sync
        def _(sp):
            sp.dma_start(b2_sb[:], b2.partition_broadcast(P)).then_inc(loaded, 16)
            sp.wait_ge(normed, 1)
            sp.dma_start(rows_by_block(x_tab), sb_x[:]).then_inc(stored, 16)
            sp.wait_ge(stored, 16)

        @block.scalar
        def _(act):
            act.wait_ge(ask, 1)
            act.activation(stat[:, 2], stat[:, 1], ACT.Sqrt).then_inc(root, 1)

        @block.vector
        def _(dve):
            step = Chain(dve, chain)
            dve.wait_ge(loaded, 16)
            step(dve.tensor_tensor(t[:], sb_x[:], y[:], ALU.add))
            step(dve.tensor_tensor(t[:], t[:], acc[:, :, 0:F], ALU.add))
            step(dve.tensor_tensor(t[:], t[:], bc(b2_sb[:], 1, NB), ALU.add))
            layer_norm(dve, step, ask, root, 0, t[:], y[:], stat, sb_x[:])
            dve.tensor_copy(stat[:, 0], stat[:, 3]).then_inc(normed, 1)


def message_out(nc, k, sb_x, acc, acc_ea, t, tmp, dis, ew1, a_tab, b_tab):
    with ExitStack() as ctx:
        st = Stage(nc, ctx, "message")
        sb, ps, sem, sems = st.sb, st.ps, st.sem, st.sems
        W = NODE_B * P
        w_ab = sb("w_ab", [F, 2, H])
        stat, part, xt = sb("stat", [P, 4, NB]), sb("part", [P, NODE_B + 1, F]), sb("xt", [F, W])
        ab = sb("ab", [P, NODE_B, 2, H])
        p_t = ps("p_t", [P, 1024])
        p_ab = ps("p_ab", [P, 8, 2, H])
        loaded, chain, ask, root = sem("loaded"), sem("chain"), sem("var_made"), sem("root_made")
        staged, turned, turned_out = sem("staged"), sem("turned"), sem("turned_out")
        ab_made, ab_out, stored = sem("ab_made"), sem("ab_out"), sem("stored")
        block = st.block()

        @block.sync
        def _(sp):
            sp.dma_start(w_ab[:], ew1[0:2 * F].rearrange("(s f) h -> f s h", s=2)).then_inc(loaded, 16)
            for i in steps(sp, NODE_STEPS):
                at = ds(i * NODE_B, NODE_B)
                sp.wait_ge(ab_out, i + 1)
                sp.dma_start(rows_by_block(a_tab)[:, at], ab[:, :, 0]).then_inc(stored, 16)
                sp.dma_start(rows_by_block(b_tab)[:, at], ab[:, :, 1]).then_inc(stored, 16)
            sp.wait_ge(stored, 32 * NODE_STEPS)

        @block.scalar
        def _(act):
            for n in range(2):
                act.wait_ge(ask, n + 1)
                act.activation(stat[:, 2], stat[:, 1], ACT.Sqrt).then_inc(root, 1)
            for i in steps(act, NODE_STEPS):
                act.wait_ge(turned, i + 1)
                act.copy(xt[:], p_t[0:F, 0:W]).then_inc(turned_out, 1)
                act.wait_ge(ab_made, i + 1)
                wait_count(act, stored, i * 32)
                act.copy(ab[:], p_ab[:, 0:NODE_B]).then_inc(ab_out, 1)

        @block.vector
        def _(dve):
            step = Chain(dve, chain)
            dve.memset(part[:, NODE_B], 0.0)
            deg = acc_ea[:, :, 2 * F]
            step(dve.tensor_scalar(stat[:, 0], deg, 0.0, None, ALU.is_gt))
            dve.tensor_scalar(stat[:, 1], deg, 1.0, None, ALU.max).then_inc(ask, 1)
            dve.wait_ge(root, 1)
            step(dve.reciprocal(stat[:, 3], stat[:, 2]))
            step(dve.tensor_tensor(dis[:], stat[:, 3], stat[:, 0], ALU.mult))
            step(dve.tensor_tensor(t[:], sb_x[:], bc(deg, 2, F), ALU.mult))
            step(dve.tensor_tensor(t[:], t[:], acc[:, :, 0:F], ALU.add))
            step(dve.tensor_tensor(t[:], t[:], acc_ea[:, :, F:2 * F], ALU.add))
            step(dve.tensor_tensor(t[:], t[:], sb_x[:], ALU.add))
            layer_norm(dve, step, ask, root, 1, t[:], tmp[:], stat, sb_x[:])
            for i in steps(dve, NODE_STEPS):
                wait_count(dve, turned, i)
                dve.tensor_copy(part[:, 0:NODE_B], sb_x[:, ds(i * NODE_B, NODE_B)]).then_inc(staged, 1)

        @block.tensor
        def _(pe):
            pe.wait_ge(loaded, 16)
            for i in steps(pe, NODE_STEPS):
                pe.wait_ge(staged, i + 1)
                for j in range(NODE_B):
                    mm = pe.transpose(p_t[:, j * P:(j + 1) * P], pair(part, j), k["ident"][:])
                mm.then_inc(turned, 1)
                pe.wait_ge(turned_out, i + 1)
                wait_count(pe, ab_out, i)
                for j in range(NODE_B):
                    mm = pe.matmul(p_ab[:, j], xt[:, j * P:(j + 1) * P], w_ab[:], start=True, stop=True)
                mm.then_inc(ab_made, 1)


def edge_mlp(nc, k, out_rec, a_tab, b_tab, acc, ew1, eb1, ew2, eb2):
    with ExitStack() as ctx:
        st = Stage(nc, ctx, "edge_mlp")
        sb, ps, sem, sems = st.sb, st.ps, st.sem, st.sems
        far, low, blks = k["far_out"], k["low_out"], k["blk_out"]
        w_attr, w2_sb = sb("w_attr", [P, G, H]), sb("w2", [H, H])
        b1_sb, b2_rows = sb("b1", [H, 1]), sb("b2_rows", [P, H])
        b2_part, b2_split, ones_b = sb("b2_part", [P, H], BF16), sb("b2_split", [P, H], BF16), sb("ones_b", [P, P], BF16)
        hot_b, ident_b = sb("hot_b", [P, G, P], BF16), sb("ident_b", [P, P], BF16)
        recs = [sb(f"recs{s}", [P, G, OUT_REC]) for s in range(SLOTS)]
        a_blk = [sb(f"a_blk{s}", [P, G, H]) for s in range(SLOTS)]
        b_rows = [sb(f"b_rows{s}", [P, G, H]) for s in range(SLOTS)]
        hot = [sb(f"hot{s}", [P, G, P]) for s in range(SLOTS)]
        hot_t, attr_t = sb("hot_t", [P, G, P]), sb("attr_t", [P, P])
        h, m = sb("h", [H, G, P]), sb("m", [P, G, H])
        p_hot = ctx.enter_context(nc.psum_tensor("edge_mlp_p_hot", [P, 2, G, P], BF16))[:, 0]
        p_attr, p_pre, p_m = ps("p_attr", [P, 512]), ps("p_pre", [H, G, P]), ps("p_m", [P, G, H])
        p_sum = [ps(f"p_sum{q}", [P, G, H]) for q in range(2)]
        set0, loaded, acc_zero = sem("w_attr_zero"), sem("loaded"), sem("acc_zero")
        rec_in, a_in, passed, kept = sems("rec_in"), sems("a_in"), sems("passed"), sems("kept")
        b_in = k["dma_edge_mlp"]
        hot_made, summed, added = sems("hot_made"), sems("summed"), sems("added")
        turned, hot_t_out, attr_t_out = sem("turned"), sem("hot_t_out"), sem("attr_t_out")
        hot_b_made, hot_turned, split = sem("hot_b_made"), sem("hot_turned"), sem("b2_split")
        pre_made, h_made, m_pre, m_made = sem("pre_made"), sem("h_made"), sem("m_pre"), sem("m_made")
        SPLITS = 4 + 3 * 3
        lanes = out_rec.rearrange("(p c) w -> p c w", p=P)
        block = st.block()

        @block.sync
        def _(sp):
            sp.wait_ge(set0, 1)
            for c in range(G):
                sp.dma_start(w_attr[c * OUT_REC:c * OUT_REC + FE + 1, c], ew1[2 * F:2 * F + FE + 1]).then_inc(loaded, 16)
            sp.dma_start(w2_sb[:], ew2).then_inc(loaded, 16)
            sp.dma_start(b1_sb[:], eb1.rearrange("(h o) -> h o", o=1)).then_inc(loaded, 16)
            sp.wait_ge(split, 1)
            for part in range(3):
                sp.dma_start(b2_rows[32 * part:32 * part + 1], eb2.rearrange("(o h) -> o h", o=1)).then_inc(loaded, 16)
            for it in steps(sp, ITERS):
                for s in range(SLOTS):
                    wait_count(sp, kept[s], it * 2)
                    wait_count(sp, summed[s], it)
                    sp.dma_start(recs[s][:], lanes[:, ds(it * STEP + s * G, G), :]).then_inc(rec_in[s], 16)
                    for c, b in enumerate(block_ids(nc, SP, blks, it, s)):
                        sp.dma_start(a_blk[s][:, c:c + 1], rows_by_block(a_tab)[:, ds(b, 1)]).then_inc(a_in[s], 16)

        @block.gpsimd
        def _(pool):
            for it in steps(pool, ITERS):
                for s in range(SLOTS):
                    pool.wait_ge(rec_in[s], it * 16 + 16)
                    turnstile(pool, k["gate"], s, passed[s])
                    for c in range(G):
                        pool.indirect_dma_start(
                            out=b_rows[s][:, c], out_offset=None, in_=b_tab,
                            in_offset=bass.IndirectOffsetOnAxis(ap=recs[s][:, c, FE + 1:FE + 2].bitcast(I32), axis=0),
                        ).then_inc(b_in[s], 16)

        def skewed(eng, body):
            for it in steps(eng, ITERS):
                for s in range(SLOTS):
                    body(it, s, s if isinstance(it, int) else SLOTS)

        def before(it, s, by):
            return (it, s - by) if s >= by else (it - 1, s - by + SLOTS)

        @block.tensor
        def _(pe):
            pe.wait_ge(loaded, 16 * (G + 5))
            pe.wait_ge(split, SPLITS)

            def second(it, s):
                pe.wait_ge(h_made, it * SLOTS + s + 1)
                for c in range(G):
                    pe.matmul(p_m[:, c], h[:, c], w2_sb[:], start=True, stop=False)
                    mm = pe.matmul(p_m[:, c], ones_b[:], b2_split[:], start=False, stop=True)
                mm.then_inc(m_pre, 1)

            def total(it, s):
                pe.wait_ge(m_made, it * SLOTS + s + 1)
                q = (s - 2) % SLOTS
                wait_count(pe, added[q], (it * G + G) if s >= 2 else it * G)
                for c in range(G):
                    mm = pe.matmul(p_sum[s % 2][:, c], hot[s][:, c], m[:, c], start=True, stop=True)
                mm.then_inc(summed[s], 1)

            def body(it, s, done):
                pe.wait_ge(rec_in[s], it * 16 + 16)
                pe.wait_ge(hot_made[s], it + 1)
                wait_count(pe, hot_t_out, it * SLOTS + s)
                wait_count(pe, attr_t_out, it * SLOTS + s)
                pe.wait_ge(hot_b_made, it * SLOTS + s + 1)
                for c in range(G):
                    tr = pe.transpose(p_hot[:, c], hot_b[:, c], ident_b[:])
                tr.then_inc(hot_turned, 1)
                pe.transpose(p_attr[:, 0:P], recs[s][:].rearrange("p c w -> p (c w)"), k["ident"][:]).then_inc(turned, 1)
                if done >= 1:
                    second(*before(it, s, 1))
                pe.wait_ge(hot_t_out, it * SLOTS + s + 1)
                pe.wait_ge(attr_t_out, it * SLOTS + s + 1)
                pe.wait_ge(a_in[s], it * (16 * G) + 16 * G)
                pe.wait_ge(b_in[s], it * (16 * G) + 16 * G)
                for c in range(G):
                    pe.matmul(p_pre[:, c], a_blk[s][:, c], hot_t[:, c], start=True, stop=False)
                    pe.matmul(p_pre[:, c], b_rows[s][:, c], k["ident"][:], start=False, stop=False)
                    mm = pe.matmul(p_pre[:, c], w_attr[:, c], attr_t[:], start=False, stop=True)
                mm.then_inc(pre_made, 1)
                if done >= 1:
                    total(*before(it, s, 1))

            skewed(pe, body)
            second(ITERS - 1, SLOTS - 1)
            total(ITERS - 1, SLOTS - 1)

        @block.scalar
        def _(act):
            act.wait_ge(loaded, 16 * (G + 5))

            def message(it, s):
                act.wait_ge(m_pre, it * SLOTS + s + 1)
                wait_count(act, summed[(s - 1) % SLOTS], it if s == 0 else it + 1)
                act.activation(m[:], p_m[:], ACT.Silu).then_inc(m_made, 1)

            def body(it, s, done):
                at = ds(it * STEP + s * G, G)
                act.wait_ge(rec_in[s], it * 16 + 16)
                act.wait_ge(passed[s], it + 1)
                act.copy(far[:, at], recs[s][:, :, FE + 1].bitcast(I32)).then_inc(kept[s], 1)
                act.copy(low[:, at], recs[s][:, :, FE + 2]).then_inc(kept[s], 1)
                act.wait_ge(turned, it * SLOTS + s + 1)
                wait_count(act, pre_made, it * SLOTS + s)
                act.copy(attr_t[:], p_attr[:, 0:P]).then_inc(attr_t_out, 1)
                if done >= 1:
                    message(*before(it, s, 1))
                act.wait_ge(pre_made, it * SLOTS + s + 1)
                act.activation(h[:], p_pre[:], ACT.Silu, bias=b1_sb[:, 0:1]).then_inc(h_made, 1)

            skewed(act, body)
            message(ITERS - 1, SLOTS - 1)

        @block.vector
        def _(dve):
            dve.memset(w_attr[:], 0.0).then_inc(set0, 1)
            step = Chain(dve, split)
            step(dve.memset(b2_rows[:], 0.0))
            step(dve.memset(b2_split[:], 0.0))
            step(dve.memset(ones_b[:], 1.0))
            step(dve.tensor_copy(ident_b[:], k["ident"][:]))
            dve.wait_ge(loaded, 16 * (G + 5))
            for part in range(3):
                row = slice(32 * part, 32 * part + 1)
                step(dve.tensor_copy(b2_part[:], b2_rows[:]))
                step(dve.tensor_copy(b2_split[row], b2_part[row]))
                step(dve.tensor_tensor(b2_rows[:], b2_rows[:], b2_part[:], ALU.subtract))
            assert step.n == SPLITS
            dve.memset(acc[:, :, 0:H], 0.0).then_inc(acc_zero, 1)
            dve.wait_ge(acc_zero, 1)

            def body(it, s, done):
                dve.wait_ge(rec_in[s], it * 16 + 16)
                dve.tensor_tensor(hot[s][:], bc(k["iota"][:], 1, G), bc(recs[s][:, :, FE + 2], 2, P),
                                  ALU.is_equal).then_inc(hot_made[s], 1)
                wait_count(dve, hot_turned, it * SLOTS + s)
                dve.wait_ge(hot_made[s], it + 1)
                dve.tensor_copy(hot_b[:], hot[s][:]).then_inc(hot_b_made, 1)
                dve.wait_ge(hot_turned, it * SLOTS + s + 1)
                wait_count(dve, pre_made, it * SLOTS + s)
                dve.tensor_copy(hot_t[:], p_hot[:]).then_inc(hot_t_out, 1)
                if done >= 2:
                    pit, q = before(it, s, 2)
                    add_to_blocks(nc, dve, block_ids(nc, DVE, blks, pit, q), acc, p_sum[q % 2], H, pit, q, summed[q], added)

            skewed(dve, body)
            for q in (SLOTS - 2, SLOTS - 1):
                add_to_blocks(nc, dve, block_ids(nc, DVE, blks, ITERS - 1, q), acc, p_sum[q % 2], H, ITERS - 1, q, summed[q], added)


def node_mlp(nc, k, sb_x, acc, t, tmp, dis, z, nw1, nb1, nw2, nb2, z_tab):
    with ExitStack() as ctx:
        st = Stage(nc, ctx, "node_mlp")
        sb, ps, sem, sems = st.sb, st.ps, st.sem, st.sems
        W = NODE_B * P
        w1x, w1a, b1_sb, w2_sb, b2_sb = sb("w1x", [F, H]), sb("w1a", [H, H]), sb("b1", [H, 1]), sb("w2", [H, F]), sb("b2", [P, F])
        stat, x_part, a_part = sb("stat", [P, 4, NB]), sb("x_part", [P, NODE_B + 1, F]), sb("a_part", [P, NODE_B, H])
        xt, at_, ut = sb("xt", [F, W]), sb("at", [H, W]), sb("ut", [H, W])
        p_x = ps("p_x", [P, 1024])
        p_a = ps("p_a", [H, 1024])
        p_u = ps("p_u", [H, 1024])
        p_y = ps("p_y", [P, NODE_B, F])
        loaded, chain, ask, root = sem("loaded"), sem("chain"), sem("var_made"), sem("root_made")
        staged, turned, turned_out, u_made = sem("staged"), sem("turned"), sem("turned_out"), sem("u_made")
        silu_made, y_made, y_kept, z_made, stored = sem("silu_made"), sem("y_made"), sem("y_kept"), sem("z_made"), sem("stored")
        block = st.block()

        @block.sync
        def _(sp):
            sp.dma_start(w1x[:], nw1[0:F]).then_inc(loaded, 16)
            sp.dma_start(w1a[:], nw1[F:F + H]).then_inc(loaded, 16)
            sp.dma_start(b1_sb[:], nb1.rearrange("(h o) -> h o", o=1)).then_inc(loaded, 16)
            sp.dma_start(w2_sb[:], nw2).then_inc(loaded, 16)
            sp.dma_start(b2_sb[:], nb2.partition_broadcast(P)).then_inc(loaded, 16)
            sp.wait_ge(z_made, 2)
            sp.dma_start(rows_by_block(z_tab), z).then_inc(stored, 16)
            sp.wait_ge(stored, 16)

        @block.scalar
        def _(act):
            act.wait_ge(loaded, 80)
            for i in steps(act, NODE_STEPS):
                act.wait_ge(turned, i + 1)
                act.copy(xt[:], p_x[0:F, 0:W]).then_inc(turned_out, 1)
                act.copy(at_[:], p_a[:, 0:W]).then_inc(turned_out, 1)
                act.wait_ge(u_made, i + 1)
                act.activation(ut[:], p_u[:, 0:W], ACT.Silu, bias=b1_sb[:, 0:1]).then_inc(silu_made, 1)
            act.wait_ge(ask, 1)
            act.activation(stat[:, 2], stat[:, 1], ACT.Sqrt).then_inc(root, 1)

        @block.tensor
        def _(pe):
            pe.wait_ge(loaded, 80)
            for i in steps(pe, NODE_STEPS):
                pe.wait_ge(staged, i * 2 + 2)
                for j in range(NODE_B):
                    pe.transpose(p_x[:, j * P:(j + 1) * P], pair(x_part, j), k["ident"][:])
                for j in range(NODE_B):
                    mm = pe.transpose(p_a[:, j * P:(j + 1) * P], a_part[:, j], k["ident"][:])
                mm.then_inc(turned, 1)
                pe.wait_ge(turned_out, i * 2 + 2)
                for lo, hi in ((0, 512), (512, W)):
                    pe.matmul(p_u[:, lo:hi], w1x[:], xt[:, lo:hi], start=True, stop=False)
                    mm = pe.matmul(p_u[:, lo:hi], w1a[:], at_[:, lo:hi], start=False, stop=True)
                mm.then_inc(u_made, 1)
                pe.wait_ge(silu_made, i + 1)
                wait_count(pe, y_kept, i)
                for j in range(NODE_B):
                    mm = pe.matmul(p_y[:, j], ut[:, j * P:(j + 1) * P], w2_sb[:], start=True, stop=True)
                mm.then_inc(y_made, 1)

        @block.vector
        def _(dve):
            step = Chain(dve, chain)
            dve.memset(x_part[:, NODE_B], 0.0)
            dve.wait_ge(loaded, 80)
            for i in steps(dve, NODE_STEPS):
                blocks = ds(i * NODE_B, NODE_B)
                wait_count(dve, turned, i)
                dve.tensor_copy(x_part[:, 0:NODE_B], sb_x[:, blocks]).then_inc(staged, 1)
                dve.tensor_copy(a_part[:], acc[:, blocks, 0:H]).then_inc(staged, 1)
                dve.wait_ge(y_made, i + 1)
                dve.tensor_tensor(t[:, blocks], p_y[:], bc(b2_sb[:], 1, NODE_B), ALU.add).then_inc(y_kept, 1)
            dve.wait_ge(y_kept, NODE_STEPS)
            step(dve.scalar_tensor_tensor(out=t[:], in0=sb_x[:], scalar=2.0, in1=t[:], op0=ALU.mult, op1=ALU.add))
            layer_norm(dve, step, ask, root, 0, t[:], tmp[:], stat, sb_x[:])
            dve.tensor_tensor(z[:, :, 0:F], sb_x[:], bc(dis[:], 2, F), ALU.mult).then_inc(z_made, 1)
            dve.tensor_copy(z[:, :, F], dis[:]).then_inc(z_made, 1)


def filter_out(nc, k, sb_x, acc, t, tmp, dis, w1t, b1, w2t, b2, out):
    with ExitStack() as ctx:
        st = Stage(nc, ctx, "filter")
        sb, ps, sem, sems = st.sb, st.ps, st.sem, st.sems
        W = NODE_B * P
        w, bias, bias2 = sb("w", [2 * F, F]), sb("bias", [P, F]), sb("bias2", [P, F])
        stat, part, pt = sb("stat", [P, 4, NB]), sb("part", [P, NODE_B, 2 * F]), sb("pt", [2 * F, W])
        p_t = ps("p_t", [P, 1024])
        p_y = ps("p_y", [P, NODE_B, F])
        loaded, chain, ask, root = sem("loaded"), sem("chain"), sem("var_made"), sem("root_made")
        staged, turned, turned_out, y_made, y_kept = sem("staged"), sem("turned"), sem("turned_out"), sem("y_made"), sem("y_kept")
        normed, stored = sem("normed"), sem("stored")
        block = st.block()

        @block.sync
        def _(sp):
            sp.dma_start(w[0:F], w1t).then_inc(loaded, 16)
            sp.dma_start(w[F:2 * F], w2t).then_inc(loaded, 16)
            sp.dma_start(bias[:], b1.partition_broadcast(P)).then_inc(loaded, 16)
            sp.dma_start(bias2[:], b2.partition_broadcast(P)).then_inc(loaded, 16)
            sp.wait_ge(normed, 1)
            full = NB - 1
            sp.dma_start(out[0:full * P].rearrange("(b p) f -> p b f", p=P), t[:, 0:full]).then_inc(stored, 16)
            sp.dma_start(out[full * P:N], t[0:TAIL, full]).then_inc(stored, 16)
            sp.wait_ge(stored, 32)

        @block.scalar
        def _(act):
            for i in steps(act, NODE_STEPS):
                act.wait_ge(turned, i + 1)
                act.copy(pt[:], p_t[:, 0:W]).then_inc(turned_out, 1)
            act.wait_ge(ask, 1)
            act.activation(stat[:, 2], stat[:, 1], ACT.Sqrt).then_inc(root, 1)

        @block.tensor
        def _(pe):
            pe.wait_ge(loaded, 64)
            for i in steps(pe, NODE_STEPS):
                pe.wait_ge(staged, i * 2 + 2)
                for j in range(NODE_B):
                    mm = pe.transpose(p_t[:, j * P:(j + 1) * P], part[:, j], k["ident"][:])
                mm.then_inc(turned, 1)
                pe.wait_ge(turned_out, i + 1)
                wait_count(pe, y_kept, i)
                for j in range(NODE_B):
                    mm = pe.matmul(p_y[:, j], pt[:, j * P:(j + 1) * P], w[:], start=True, stop=True)
                mm.then_inc(y_made, 1)

        @block.vector
        def _(dve):
            step = Chain(dve, chain)
            dve.wait_ge(loaded, 64)
            step(dve.tensor_tensor(bias[:], bias[:], bias2[:], ALU.add))
            for i in steps(dve, NODE_STEPS):
                blocks = ds(i * NODE_B, NODE_B)
                wait_count(dve, turned, i)
                dve.tensor_copy(part[:, :, 0:F], acc[:, blocks, 0:F]).then_inc(staged, 1)
                dve.tensor_tensor(part[:, :, F:2 * F], acc[:, blocks, 0:F], sb_x[:, blocks], ALU.mult).then_inc(staged, 1)
                dve.wait_ge(y_made, i + 1)
                dve.tensor_copy(t[:, blocks], p_y[:]).then_inc(y_kept, 1)
            dve.wait_ge(y_kept, NODE_STEPS)
            step(dve.tensor_tensor(tmp[:], bc(bias[:], 1, NB), bc(acc[:, :, F], 2, F), ALU.mult))
            step(dve.tensor_tensor(t[:], t[:], tmp[:], ALU.add))
            step(dve.tensor_tensor(t[:], t[:], bc(dis[:], 2, F), ALU.mult))
            step(dve.scalar_tensor_tensor(out=tmp[:], in0=t[:], scalar=0.2, in1=t[:], op0=ALU.mult, op1=ALU.max))
            step(dve.tensor_tensor(t[:], tmp[:], sb_x[:], ALU.add))
            layer_norm(dve, step, ask, root, 0, t[:], tmp[:], stat, tmp[:])
            dve.tensor_copy(t[:], tmp[:]).then_inc(normed, 1)


def gnn_stack(nc, x, src, dst, ea16, ea64, weight, g_w1, g_b1, g_w2, g_b2, ew1, eb1, ew2, eb2,
              nw1, nb1, nw2, nb2, f_w1t, f_b1, f_w2t, f_b2, out):
    rows = NB * P
    in_rec = nc.dram_tensor("in_records", [E, IN_REC], F32).ap()
    out_rec = nc.dram_tensor("out_records", [P * CHUNKS, OUT_REC], F32).ap()
    y_tab, x_tab = (nc.dram_tensor(n, [rows, F], F32).ap() for n in ("y_table", "x_table"))
    a_tab, b_tab = (nc.dram_tensor(n, [rows, H], F32).ap() for n in ("a_table", "b_table"))
    z_tab = nc.dram_tensor("z_table", [rows, F + 1], F32).ap()
    with ExitStack() as ctx:
        st = Stage(nc, ctx, "nodes")
        sb, ps, sem, sems = st.sb, st.ps, st.sem, st.sems
        k = alloc_constants(nc, ctx)
        for name in ("scatter", "sum_x", "sum_y", "sum_x1", "edge_mlp", "sum_z"):
            k["dma_" + name] = [ctx.enter_context(nc.semaphore(f"dma_{name}{s}")) for s in range(SLOTS)]
        constants(nc, k)
        wide_sums, in_sums = sb("wide_sums", [P, NB + 1, 2 * F + 1]), sb("in_sums", [P, NB + 1, F])
        wide, sums = wide_sums[:, 0:NB], in_sums[:, 0:NB]
        with ExitStack() as edges_ctx:
            a = EdgeArrays(nc, edges_ctx)
            a.iota = k["iota"]
            count_edges(nc, k, a, src, dst, weight)
            sort_in(nc, k, a, ea64, in_rec)
            tables_in(nc, k, src, dst, in_rec)
            edge_sums(nc, "sum_x", k, "in", x, F, wide_sums, 2 * F + 1, attrs=(ea64, in_rec), a=a, out_rec=out_rec)
            scatter_out(nc, k, a, ea16, out_rec)
        for o in ("far_out", "low_out"):
            k[o] = sb(o, [P, CHUNKS], I32 if o == "far_out" else F32)
        node_x, node_y, node_t = (sb(n, [P, NB, F]) for n in ("node_x", "node_y", "node_t"))
        dis = sb("dis", [P, NB])
        gin_hidden(nc, k, node_x, wide, node_y, x, g_w1, g_b1, g_w2, y_tab)
        edge_sums(nc, "sum_y", k, "in", y_tab, F, in_sums, F)
        gin_out(nc, k, node_x, sums, node_y, node_t, g_b2, x_tab)
        edge_sums(nc, "sum_x1", k, "in", x_tab, F, in_sums, F)
        message_out(nc, k, node_x, sums, wide, node_t, node_y, dis, ew1, a_tab, b_tab)
        edge_mlp(nc, k, out_rec, a_tab, b_tab, wide, ew1, eb1, ew2, eb2)
        node_mlp(nc, k, node_x, wide, node_t, node_y, dis, wide[:, :, 0:F + 1], nw1, nb1, nw2, nb2, z_tab)
        edge_sums(nc, "sum_z", k, "out", z_tab, F + 1, wide, F + 1)
        filter_out(nc, k, node_x, wide, node_t, node_y, dis, f_w1t, f_b1, f_w2t, f_b2, out)


NAMES = ["x", "src", "dst", "edge_attr_16", "edge_attr_64", "edge_weight", "L0_gnn_W1", "L0_gnn_b1", "L0_gnn_W2",
         "L0_gnn_b2", "L2_gnn_ew1", "L2_gnn_eb1", "L2_gnn_ew2", "L2_gnn_eb2", "L2_gnn_nw1", "L2_gnn_nb1",
         "L2_gnn_nw2", "L2_gnn_nb2", "L3_gnn_W1", "L3_gnn_b1", "L3_gnn_W2", "L3_gnn_b2"]


def kernel(**inputs):
    import numpy as np
    import concourse.bacc as bacc
    from concourse.bass_utils import run_bass_kernel_spmd

    nc = bacc.Bacc("TRN2", target_bir_lowering=False, num_devices=1)
    arrays, args = {}, []
    for name in NAMES:
        a = np.asarray(inputs[name])
        if name in ("L3_gnn_W1", "L3_gnn_W2"):
            a = a.T
        a = np.ascontiguousarray(a)
        arrays["in_" + name] = a
        args.append(nc.dram_tensor("in_" + name, a.shape, mybir.dt.from_np(a.dtype), kind="ExternalInput").ap())
    out = nc.dram_tensor("out", (N, F), F32, kind="ExternalOutput").ap()
    gnn_stack(nc, *args, out)
    r = run_bass_kernel_spmd(nc, [arrays], core_ids=[0])
    return r.results[0]["out"]
```
